# Optimizing a Trainium2 kernel written in Bass

```python
import numpy as np
import jax
import jax.numpy as jnp

def _softmax(x, axis=-1):
    return jax.nn.softmax(x, axis=axis)

def _gelu(x):
    return jax.nn.gelu(x, approximate=True)

def _silu(x):
    return jax.nn.silu(x)

def _sigmoid(x):
    return jax.nn.sigmoid(x)

def _layernorm(x, axis=-1, eps=1e-05):
    m = jnp.mean(x, axis=axis, keepdims=True)
    v = jnp.var(x, axis=axis, keepdims=True)
    return (x - m) / jnp.sqrt(v + eps)

def _scatter_add(tgt, idx, src, axis=0):
    return tgt.at[idx].add(src)

def _segment_sum(src, seg, n):
    return jax.ops.segment_sum(src, seg, n)
kernel_name = 'mk_flamingo_gated_d1_seqx_r8_d2ca86'

def setup_inputs(seed: int=0):
    np.random.seed(seed)
    _w = jnp.asarray

    def _rec_inputs():
        import jax
        import jax.numpy as jnp
        _rk = jax.random.key(seed)
        x = -0.000125 + 0.9999 * jax.random.normal(jax.random.fold_in(_rk, 1), (2, 256, 256), jnp.float32)
        _lenS = 256 - jax.random.randint(jax.random.fold_in(_rk, 7), (2,), 0, max(1, 256 // 4) + 1, jnp.int32)
        _lenS2 = 512 - jax.random.randint(jax.random.fold_in(_rk, 8), (2,), 0, max(1, 512 // 4) + 1, jnp.int32)
        _ctx_2048P = jax.random.normal(jax.random.fold_in(_rk, 11), (2, 16, 256), jnp.float32)
        _ctx_2048c = jax.random.dirichlet(jax.random.fold_in(_rk, 511), 0.3 * jnp.ones((16,), jnp.float32), (2, 512))
        _ctx_2048t = jnp.einsum('bsk,bkd->bsd', _ctx_2048c, _ctx_2048P)
        _ctx_2048t = _ctx_2048t * jax.lax.rsqrt(jnp.mean(jnp.square(_ctx_2048t)) + 1e-12) * 0.953939
        ctx_2048 = -0.000514642 + 1.00011 * (_ctx_2048t + 0.3 * jax.random.normal(jax.random.fold_in(_rk, 611), (2, 512, 256), jnp.float32))
        _validS = jnp.arange(256)[None, :] < _lenS[:, None]
        _validS2 = jnp.arange(512)[None, :] < _lenS2[:, None]
        _causal = jnp.tril(jnp.ones((256, 256), dtype=bool))
        mask_BxS2_bk0 = jnp.logical_not(jnp.broadcast_to(_validS2[:, :], (2, 512)))
        _g = jax.random.normal(jax.random.fold_in(_rk, 9001), (2, 1), jnp.float32)
        _g = jnp.sign(_g) * jnp.maximum(jnp.abs(_g), 1.0) + (_g == 0) * 1.0
        g_xattn = _g[0]
        g_ffn = _g[1]
        return (x, ctx_2048, mask_BxS2_bk0, g_xattn, g_ffn)
    x, ctx_2048, mask_BxS2_bk0, g_xattn, g_ffn = _rec_inputs()

    def _L0_xattn_setup():
        import jax, jax.numpy as jnp
        import numpy as np
        key = jax.random.key(seed)
        k1, k2, k3 = jax.random.split(key, 3)
        B, S, D, M = (8, 256, 256, 128)
        hidden_states = jax.random.normal(k1, (B, S, D), dtype=jnp.float32)
        memory_tokens = jax.random.normal(k2, (B, M, D), dtype=jnp.float32)
        memory_mask = jax.random.randint(k3, (B, M), 0, 2).astype(jnp.bool_)
        return {'hidden_states': hidden_states, 'memory_tokens': memory_tokens, 'memory_mask': memory_mask}
    _L0_xattn_all = _L0_xattn_setup()
    _L0_xattn_in = {k: v for k, v in _L0_xattn_all.items() if k in ()}
    del _L0_xattn_all

    def _L0_ffn_setup():
        import jax, jax.numpy as jnp
        import numpy as np
        DIM = 256
        EXPERT_DIM = 128
        N_EXPERTS = 16
        TOPK = 2
        N_SHARED = 1
        B, T = (4, 256)
        key = jax.random.key(seed)
        ks = jax.random.split(key, 9)
        s = 0.02
        return {'x': jax.random.normal(ks[0], (B, T, DIM), jnp.float32), 'router_w': jax.random.normal(ks[1], (N_EXPERTS, DIM), jnp.float32) * s, 'router_bias': jnp.zeros((N_EXPERTS,), jnp.float32), 'Wu': jax.random.normal(ks[2], (N_EXPERTS, DIM, EXPERT_DIM), jnp.float32) * s, 'Wg': jax.random.normal(ks[3], (N_EXPERTS, DIM, EXPERT_DIM), jnp.float32) * s, 'Wd': jax.random.normal(ks[4], (N_EXPERTS, EXPERT_DIM, DIM), jnp.float32) * s, 'Su': jax.random.normal(ks[5], (N_SHARED, DIM, EXPERT_DIM * TOPK), jnp.float32) * s, 'Sg': jax.random.normal(ks[6], (N_SHARED, DIM, EXPERT_DIM * TOPK), jnp.float32) * s, 'Sd': jax.random.normal(ks[7], (N_SHARED, EXPERT_DIM * TOPK, DIM), jnp.float32) * s}
    _L0_ffn_all = _L0_ffn_setup()
    _L0_ffn_in = {k: v for k, v in _L0_ffn_all.items() if k in ('router_w', 'router_bias', 'Wu', 'Wg', 'Wd', 'Su', 'Sg', 'Sd')}
    del _L0_ffn_all
    return {'x': x, 'ctx_2048': ctx_2048, 'mask_BxS2_bk0': mask_BxS2_bk0, 'g_xattn': g_xattn, 'g_ffn': g_ffn, 'L0_ffn_router_w': _L0_ffn_in['router_w'], 'L0_ffn_router_bias': _L0_ffn_in['router_bias'], 'L0_ffn_Wu': _L0_ffn_in['Wu'], 'L0_ffn_Wg': _L0_ffn_in['Wg'], 'L0_ffn_Wd': _L0_ffn_in['Wd'], 'L0_ffn_Su': _L0_ffn_in['Su'], 'L0_ffn_Sg': _L0_ffn_in['Sg'], 'L0_ffn_Sd': _L0_ffn_in['Sd']}

def reference(x, ctx_2048, mask_BxS2_bk0, g_xattn, g_ffn, L0_ffn_router_w, L0_ffn_router_bias, L0_ffn_Wu, L0_ffn_Wg, L0_ffn_Wd, L0_ffn_Su, L0_ffn_Sg, L0_ffn_Sd):
    import jax
    import jax.numpy as jnp

    def _L0_xattn_ref(hidden_states, memory_tokens, memory_mask):
        import jax, jax.numpy as jnp
        import numpy as np
        B, S, D = hidden_states.shape
        scale = 1.0 / jnp.sqrt(jnp.asarray(D, hidden_states.dtype))
        scores = jnp.einsum('bsd,bmd->bsm', hidden_states, memory_tokens) * scale
        neg_inf = jnp.asarray(-1e+30, scores.dtype)
        scores = jnp.where(memory_mask[:, None, :], scores, neg_inf)
        attn = jax.nn.softmax(scores, axis=-1)
        readout = jnp.einsum('bsm,bmd->bsd', attn, memory_tokens)
        valid_b = jnp.any(memory_mask, axis=-1)
        out = jnp.where(valid_b[:, None, None], readout, jnp.zeros_like(readout))
        return out

    def _L0_ffn_ref(x, router_w, router_bias, Wu, Wg, Wd, Su, Sg, Sd):
        import jax, jax.numpy as jnp
        import numpy as np
        DIM = 256
        EXPERT_DIM = 128
        N_EXPERTS = 16
        TOPK = 2
        N_SHARED = 1
        B, T = (4, 256)
        Bx, Tx, D = x.shape
        flat = x.reshape(Bx * Tx, D)
        logits = flat @ router_w.T
        scores = jax.nn.softmax(logits, axis=-1)
        _, topk_idx = jax.lax.top_k(logits + router_bias, TOPK)
        topk_scores = jnp.take_along_axis(scores, topk_idx, axis=-1)
        topk_scores = topk_scores / topk_scores.sum(-1, keepdims=True)
        combine = jnp.einsum('nk,nke->ne', topk_scores, jax.nn.one_hot(topk_idx, N_EXPERTS, dtype=scores.dtype))
        out = jnp.zeros_like(flat)
        for e in range(N_EXPERTS):
            h = jax.nn.silu(flat @ Wu[e]) * (flat @ Wg[e])
            out = out + combine[:, e:e + 1] * (h @ Wd[e])
        for s in range(N_SHARED):
            out = out + jax.nn.silu(flat @ Su[s]) * (flat @ Sg[s]) @ Sd[s]
        return out.reshape(Bx, Tx, D)
    x = x + jnp.tanh(g_xattn[0]) * _L0_xattn_ref(_layernorm(x, axis=-1), ctx_2048, mask_BxS2_bk0)
    x = x + jnp.tanh(g_ffn[0]) * _L0_ffn_ref(_layernorm(x, axis=-1), L0_ffn_router_w, L0_ffn_router_bias, L0_ffn_Wu, L0_ffn_Wg, L0_ffn_Wd, L0_ffn_Su, L0_ffn_Sg, L0_ffn_Sd)
    return x

_drawn_inputs = setup_inputs


def setup_inputs(seed=0):
    import zlib

    import numpy as np

    out = dict(_drawn_inputs(seed))
    spreads = {'L0_ffn_router_bias': (0.0, 0.8)}
    factors = {'L0_ffn_router_w': 8.0,
     'L0_ffn_Wu': 7.787,
     'L0_ffn_Wg': 7.762,
     'L0_ffn_Wd': 7.674,
     'L0_ffn_Su': 4.004,
     'L0_ffn_Sg': 3.955,
     'L0_ffn_Sd': 3.929}
    for name, (base, spread) in spreads.items():
        noise = np.random.default_rng([zlib.crc32(name.encode()), seed]).standard_normal(out[name].shape)
        drawn = base * np.exp(spread * noise) if base else spread * noise
        out[name] = jnp.asarray(drawn.astype(out[name].dtype))
    for name, factor in factors.items():
        out[name] = (out[name] * factor).astype(out[name].dtype)
    return out
```

```python
from contextlib import ExitStack

import concourse.bass as bass
from concourse import mybir

F32 = mybir.dt.float32
F32R = mybir.dt.float32r
BF16 = mybir.dt.bfloat16
ALU = mybir.AluOpType
ACT = mybir.ActivationFunctionType
AX = mybir.AxisListType

P = 128
MASKED = -1e30
EPS = 1e-5


def flamingo_block(nc, x, ctx_mem, mask, g_xattn, g_ffn, router_w, router_b, Wu, Wg, Wd, Su, Sg, Sd, out):
    B, S, D = x.shape
    M = ctx_mem.shape[1]
    E, _, F = Wu.shape
    NK = D // P
    NT = B * S // P
    TB = S // P
    NM = M // P
    NS = Su.shape[2] // F
    NE = NS + E
    WUG = 2 * NK * F
    WW = WUG + D
    SCALE = float(D) ** -0.5
    assert NK == 2 and TB == 2 and F == P and NS == 2 and B == 2

    x_v = x.rearrange("b (t p) d -> b p t d", p=P)
    out_v = out.rearrange("b (t p) d -> (b t) p d", p=P)
    ctx_v = ctx_mem.rearrange("b (m p) d -> b p m d", p=P)

    with ExitStack() as stack:
        def sb(name, shape, dt=F32):
            return stack.enter_context(nc.sbuf_tensor(name, shape, dt))

        def sem(name):
            return stack.enter_context(nc.semaphore(name))

        bank = [stack.enter_context(nc.psum_tensor(f"bank{i}", [P, 512], F32)) for i in range(8)]
        SCORE_BANK = [6, 7, 0, 1]
        PT_BANK = [2, 3, 4, 5]
        U_BANK, G_BANK = [0, 1], [6, 7]
        Y_BANK = [[2, 3], [4, 5]]

        ident = sb("ident", [P, P])
        ones_row = sb("ones_row", [P, P], BF16)
        neg_half = sb("neg_half", [P, NT])
        rank = sb("rank", [P, E])
        x_sb = sb("x_sb", [P, NT, D])
        ctx_sb = sb("ctx_sb", [P, B * NM, D])
        mask_sb = sb("mask_sb", [P, B, M], mybir.dt.uint8)
        gates = sb("gates", [P, 2])
        rw_sb = sb("rw_sb", [E, D])
        rb_sb = sb("rb_sb", [P, E])
        w_raw = sb("w_raw", [P, NE, WW])
        mask_bias = sb("mask_bias", [P, B, M], BF16)
        valid = sb("valid", [P, B])
        stats = sb("stats", [P, NT, 6])
        mean_var = sb("mean_var", [P, NT, 2])
        var_eps = sb("var_eps", [P, NT])
        rstd = sb("rstd", [P, NT])
        xn = sb("xn", [P, NT, D])
        xT_hi = sb("xT_hi", [P, B, NK, S], F32R)
        xT_lo = sb("xT_lo", [P, B, NK, S], F32R)
        ctxT_hi = sb("ctxT_hi", [P, B * NK, M], F32R)
        ctxT_lo = sb("ctxT_lo", [P, B * NK, M], F32R)
        ctx_hi = sb("ctx_hi", [P, B * NM, D], F32R)
        ctx_lo = sb("ctx_lo", [P, B * NM, D], F32R)
        row_max = sb("row_max", [P, NT])
        exp_bias = sb("exp_bias", [P, NT])
        probs = sb("probs", [P, NT, M])
        row_sum = sb("row_sum", [P, NT])
        inv_sum = sb("inv_sum", [P, NT])
        tanh_g = sb("tanh_g", [P, 2])
        gate_valid = sb("gate_valid", [P, B])
        coef = sb("coef", [P, NT])
        pT_hi = sb("pT_hi", [P, NT, NM, P], F32R)
        pT_lo = sb("pT_lo", [P, NT, NM, P], F32R)
        x1 = sb("x1", [P, NT, D])
        stats2 = sb("stats2", [P, NT, 6])
        mean_var2 = sb("mean_var2", [P, NT, 2])
        var_eps2 = sb("var_eps2", [P, NT])
        rstd2 = sb("rstd2", [P, NT])
        xn2 = sb("xn2", [P, NT, D])
        fT_hi = sb("fT_hi", [P, B, NK, S], F32R)
        fT_lo = sb("fT_lo", [P, B, NK, S], F32R)
        rwT_hi = sb("rwT_hi", [P, NK, E], F32R)
        rwT_lo = sb("rwT_lo", [P, NK, E], F32R)
        logits = sb("logits", [P, NT, E])
        biased = sb("biased", [P, NT, E])
        rest = sb("rest", [P, NT, E])
        at_max = sb("at_max", [P, NT, E])
        first = sb("first", [P, NT, E])
        second = sb("second", [P, NT, E])
        top = sb("top", [P, NT])
        top_rank = sb("top_rank", [P, NT])
        logit_max = sb("logit_max", [P, NT])
        centred = sb("centred", [P, NT, E])
        expd = sb("expd", [P, NT, E])
        total = sb("total", [P, NT])
        inv_total = sb("inv_total", [P, NT])
        comb = sb("comb", [P, NT, NE])
        wug_hi = sb("wug_hi", [P, 2, WUG], F32R)
        wug_lo = sb("wug_lo", [P, 2, WUG], F32R)
        wd_hi = sb("wd_hi", [P, 2, D], F32R)
        wd_lo = sb("wd_lo", [P, 2, D], F32R)
        silu = sb("silu", [P, 2, NT * P])
        h = sb("h", [P, 2, NT * P])
        h_hi = sb("h_hi", [P, 2, NT * P], F32R)
        h_lo = sb("h_lo", [P, 2, NT * P], F32R)
        acc = sb("acc", [P, NT, D])
        result = sb("result", [P, NT, D])

        x_landed = [sem(f"x_landed{b}") for b in range(B)]
        ctx_landed = [sem(f"ctx_landed{b}") for b in range(B)]
        small_landed = sem("small_landed")
        w_landed = [sem(f"w_landed{p}") for p in range(2)]
        out_stored = sem("out_stored")
        pool_step = sem("pool_step")
        consts_ready = sem("consts_ready")
        mask_ready = sem("mask_ready")
        dve_step = sem("dve_step")
        var_ready = sem("var_ready")
        rstd_ready = sem("rstd_ready")
        xn_ready = sem("xn_ready")
        turned = sem("turned")
        hi_ready = sem("hi_ready")
        lo_ready = sem("lo_ready")
        ctx_split = sem("ctx_split")
        ctx_hi_ready = sem("ctx_hi_ready")
        scores_ready = sem("scores_ready")
        bias_ready = sem("bias_ready")
        probs_ready = sem("probs_ready")
        tanh_ready = sem("tanh_ready")
        read_ready = sem("read_ready")
        x1_ready = sem("x1_ready")
        logits_ready = sem("logits_ready")
        centred_ready = sem("centred_ready")
        expd_ready = sem("expd_ready")
        u_done, g_done, y_done = sem("u_done"), sem("g_done"), sem("y_done")
        silu_done, mul_done = sem("silu_done"), sem("mul_done")
        h_hi_done, h_lo_done = sem("h_hi_done"), sem("h_lo_done")
        wug_hi_done, wug_lo_done = sem("wug_hi_done"), sem("wug_lo_done")
        wd_hi_done, wd_lo_done = sem("wd_hi_done"), sem("wd_lo_done")
        acc_done = sem("acc_done")
        result_ready = sem("result_ready")

        def view(i, n=512):
            return bank[i][:, 0:n]

        splits = [(view(2 + k), ctxT_hi[:, k, :], ctxT_lo[:, k, :]) for k in range(NK)]
        splits += [(view(6, NK * E), rwT_hi[:].rearrange("p k e -> p (k e)"), rwT_lo[:].rearrange("p k e -> p (k e)"))]
        splits += [(view(b), xT_hi[:, b].rearrange("p k s -> p (k s)"), xT_lo[:, b].rearrange("p k s -> p (k s)"))
                   for b in range(B)]
        splits += [(view(4 + k), ctxT_hi[:, NK + k, :], ctxT_lo[:, NK + k, :]) for k in range(NK)]
        FIRST_PT = len(splits)
        splits += [(view(PT_BANK[t]), pT_hi[:, t].rearrange("p m s -> p (m s)"),
                    pT_lo[:, t].rearrange("p m s -> p (m s)")) for t in range(NT)]
        FIRST_F = len(splits)
        splits += [(view(2 + b), fT_hi[:, b].rearrange("p k s -> p (k s)"), fT_lo[:, b].rearrange("p k s -> p (k s)"))
                   for b in range(B)]

        block = stack.enter_context(nc.Block())

        @block.sync
        def _(sp):
            sp.dma_start(x_sb[:, 0:TB, :], x_v[0]).then_inc(x_landed[0], 16)
            sp.dma_start(ctx_sb[:, 0:NM, :], ctx_v[0]).then_inc(ctx_landed[0], 16)
            sp.dma_start(x_sb[:, TB:NT, :], x_v[1]).then_inc(x_landed[1], 16)
            sp.dma_start(ctx_sb[:, NM:2 * NM, :], ctx_v[1]).then_inc(ctx_landed[1], 16)
            for j in range(NS):
                cols = slice(j * F, (j + 1) * F)
                for n, w in enumerate((Su, Sg)):
                    sp.dma_start(w_raw[:, j, n * NK * F:(n + 1) * NK * F].rearrange("p (k f) -> p k f", k=NK),
                                 w[0, :, cols].rearrange("(k p) f -> p k f", p=P)).then_inc(w_landed[j % 2], 16)
                sp.dma_start(w_raw[:, j, WUG:WW], Sd[0, cols, :]).then_inc(w_landed[j % 2], 16)
            with sp.Fori(0, E // 2) as i:
                for par in range(2):
                    e = 2 * i + par
                    sp.wait_ge(w_landed[par], 48 * i + 48)
                    for n, w in enumerate((Wu, Wg)):
                        sp.dma_start(
                            w_raw[:, bass.ds(e + NS, 1), n * NK * F:(n + 1) * NK * F].rearrange(
                                "p o (k f) -> p (o k) f", k=NK),
                            w[bass.ds(e, 1), :, :].rearrange("o (k p) f -> p (o k) f", p=P),
                        ).then_inc(w_landed[par], 16)
                    sp.dma_start(w_raw[:, bass.ds(e + NS, 1), WUG:WW],
                                 Wd[bass.ds(e, 1), :, :].rearrange("o p d -> p o d")).then_inc(w_landed[par], 16)
            for t in range(NT):
                sp.wait_ge(result_ready, t + 1)
                sp.dma_start(out_v[t], result[:, t, :]).then_inc(out_stored, 16)
            sp.wait_ge(out_stored, 16 * NT)

        @block.gpsimd
        def _(pool):
            pool.memset(ident[:], 1.0).then_inc(pool_step, 1)
            pool.wait_ge(pool_step, 1)
            pool.affine_select(out=ident[:], in_=ident[:], compare_op=ALU.is_equal, fill=0.0, base=0,
                               pattern=[[-1, P]], channel_multiplier=1).then_inc(consts_ready, 1)
            pool.memset(neg_half[:], -0.5).then_inc(consts_ready, 1)
            pool.memset(ones_row[:], 1.0).then_inc(pool_step, 1)
            pool.wait_ge(pool_step, 2)
            pool.affine_select(out=ones_row[:], in_=ones_row[:], compare_op=ALU.is_equal, fill=0.0, base=0,
                               pattern=[[0, P]], channel_multiplier=1).then_inc(consts_ready, 1)
            pool.iota(rank[:], pattern=[[-1, E]], base=E, channel_multiplier=0,
                      allow_small_or_imprecise_dtypes=True).then_inc(consts_ready, 1)
            pool.memset(acc[:], 0.0).then_inc(acc_done, 1)
            pool.memset(comb[:], 1.0).then_inc(consts_ready, 1)
            for b in range(B):
                pool.wait_ge(var_ready, b + 1)
                pool.tensor_tensor(rstd[:, TB * b:TB * b + TB], var_eps[:, TB * b:TB * b + TB],
                                   neg_half[:, TB * b:TB * b + TB], ALU.pow).then_inc(rstd_ready, 1)
            for b in range(B):
                rows = slice(NM * b, NM * b + NM)
                pool.wait_ge(ctx_hi_ready, b + 1)
                pool.tensor_tensor(ctx_lo[:, rows, :], ctx_sb[:, rows, :], ctx_hi[:, rows, :].bitcast(F32),
                                   ALU.subtract).then_inc(ctx_split, 1)

            def wug_low(e, par):
                pool.wait_ge(wug_hi_done, e + 1)
                pool.tensor_tensor(wug_lo[:, par, :], w_raw[:, bass.ds(e, 1), 0:WUG],
                                   wug_hi[:, par, :].bitcast(F32), ALU.subtract).then_inc(wug_lo_done, 1)

            def wd_low(e, par):
                pool.wait_ge(wd_hi_done, e + 1)
                pool.tensor_tensor(wd_lo[:, par, :], w_raw[:, bass.ds(e, 1), WUG:WW],
                                   wd_hi[:, par, :].bitcast(F32), ALU.subtract).then_inc(wd_lo_done, 1)

            wug_low(0, 0)
            wug_low(1, 1)
            wd_low(0, 0)
            for t in range(NT):
                pool.wait_ge(var_ready, B + t + 1)
                pool.tensor_tensor(rstd2[:, t:t + 1], var_eps2[:, t:t + 1], neg_half[:, t:t + 1],
                                   ALU.pow).then_inc(rstd_ready, 1)

            def step(e, par):
                wug_low(e + 2, par)
                wd_low(e + 1, 1 - par)

            step(0, 0)
            with pool.Fori(0, (NE - 4) // 2) as i:
                step(2 * i + 1, 1)
                step(2 * i + 2, 0)
            step(NE - 3, 1)
            wd_low(NE - 1, 1)

        @block.scalar
        def _(act):
            act.dma_start(gates[:, 0:1], g_xattn.rearrange("(o n) -> o n", o=1).broadcast_to([P, 1])).then_inc(small_landed, 16)
            act.dma_start(gates[:, 1:2], g_ffn.rearrange("(o n) -> o n", o=1).broadcast_to([P, 1])).then_inc(small_landed, 16)
            act.dma_start(mask_sb[:].rearrange("p b m -> p (b m)"),
                          mask.rearrange("(o b) m -> o (b m)", o=1).broadcast_to([P, B * M])).then_inc(small_landed, 16)
            act.dma_start(rb_sb[:], router_b.rearrange("(o n) -> o n", o=1).broadcast_to([P, E])).then_inc(small_landed, 16)
            act.dma_start(rw_sb[:], router_w).then_inc(small_landed, 16)

            def high(n):
                src, hi, _ = splits[n]
                act.wait_ge(turned, n + 1)
                act.copy(hi, src).then_inc(hi_ready, 1)

            high(0)
            high(1)
            high(2)
            high(3)
            act.wait_ge(ctx_landed[0], 16)
            act.copy(ctx_hi[:, 0:NM, :], ctx_sb[:, 0:NM, :]).then_inc(ctx_hi_ready, 1)
            high(4)
            high(5)
            high(6)

            def exponentials(t):
                act.wait_ge(bias_ready, t + 1)
                act.activation(probs[:, t, :], view(SCORE_BANK[t]), ACT.Exp, bias=exp_bias[:, t:t + 1],
                               scale=SCALE, accum_out=row_sum[:, t:t + 1]).then_inc(probs_ready, 1)

            act.wait_ge(small_landed, 5 * 16)
            act.activation(tanh_g[:], gates[:], ACT.Tanh).then_inc(tanh_ready, 1)
            exponentials(0)
            exponentials(1)
            high(FIRST_PT)
            exponentials(2)
            act.wait_ge(ctx_landed[1], 16)
            act.copy(ctx_hi[:, NM:2 * NM, :], ctx_sb[:, NM:2 * NM, :]).then_inc(ctx_hi_ready, 1)
            high(FIRST_PT + 1)
            exponentials(3)
            high(FIRST_PT + 2)
            high(FIRST_PT + 3)

            def wug_high(e, par, after, count):
                act.wait_ge(w_landed[par], count)
                if after is not None:
                    act.wait_ge(g_done, after)
                act.copy(wug_hi[:, par, :], w_raw[:, bass.ds(e, 1), 0:WUG]).then_inc(wug_hi_done, 1)

            def wd_high(e, par, after):
                if after is not None:
                    act.wait_ge(y_done, after)
                act.copy(wd_hi[:, par, :], w_raw[:, bass.ds(e, 1), WUG:WW]).then_inc(wd_hi_done, 1)

            wug_high(0, 0, None, 48)
            wug_high(1, 1, None, 48)
            wd_high(0, 0, None)
            high(FIRST_F)
            high(FIRST_F + 1)
            act.wait_ge(centred_ready, 1)
            act.activation(expd[:], centred[:], ACT.Exp).then_inc(expd_ready, 1)

            def step(e, par, landed=None, more=2, lead=False):
                act.wait_ge(u_done, e + 1)
                act.activation(silu[:, par, :], view(U_BANK[par]), ACT.Silu).then_inc(silu_done, 1)
                if more == 2:
                    wug_high(e + 2, par, e + 1, landed)
                act.wait_ge(mul_done, e + 1)
                act.copy(h_hi[:, par, :], h[:, par, :]).then_inc(h_hi_done, 1)
                if more >= 1:
                    wd_high(e + 1, 1 - par, None if lead else e)

            step(0, 0, 96, lead=True)
            with act.Fori(0, (NE - 4) // 2) as i:
                step(2 * i + 1, 1, 48 * i + 96)
                step(2 * i + 2, 0, 48 * i + 144)
            step(NE - 3, 1, 48 * (NE // 2))
            step(NE - 2, 0, more=1)
            step(NE - 1, 1, more=0)

        @block.vector
        def _(dve):
            steps = [0]

            def link(ins):
                steps[0] += 1
                ins.then_inc(dve_step, 1)
                dve.wait_ge(dve_step, steps[0])

            def low(n):
                src, hi, lo = splits[n]
                dve.wait_ge(hi_ready, n + 1)
                dve.tensor_tensor(lo, src, hi.bitcast(F32), ALU.subtract).then_inc(lo_ready, 1)

            def moments(b):
                dve.wait_ge(x_landed[b], 16)
                for t in range(TB * b, TB * b + TB):
                    link(dve.bn_stats(stats[:, t, :], x_sb[:, t, :]))
                    link(dve.bn_aggr(mean_var[:, t, :], stats[:, t, :]))
                dve.tensor_scalar(var_eps[:, TB * b:TB * b + TB], mean_var[:, TB * b:TB * b + TB, 1], EPS, None,
                                  ALU.add).then_inc(var_ready, 1)

            def normalise(b):
                dve.wait_ge(rstd_ready, b + 1)
                for t in range(TB * b, TB * b + TB):
                    dve.tensor_scalar(xn[:, t, :], x_sb[:, t, :], mean_var[:, t, 0:1], rstd[:, t:t + 1],
                                      ALU.subtract, ALU.mult).then_inc(xn_ready, 1)

            moments(0)
            dve.wait_ge(small_landed, 5 * 16)
            dve.tensor_scalar(mask_bias[:], mask_sb[:], 1.0, -MASKED / SCALE, ALU.subtract,
                              ALU.mult).then_inc(mask_ready, 1)
            link(dve.tensor_reduce(valid[:], mask_sb[:], AX.X, ALU.max))
            normalise(0)
            low(0)
            low(1)
            low(2)
            moments(1)
            low(3)
            normalise(1)
            low(4)
            low(5)
            low(6)
            dve.wait_ge(tanh_ready, 1)
            link(dve.tensor_scalar(gate_valid[:], valid[:], tanh_g[:, 0:1], None, ALU.mult))

            def maximum(t):
                dve.wait_ge(scores_ready, t + 1)
                link(dve.tensor_reduce(row_max[:, t:t + 1], view(SCORE_BANK[t]), AX.X, ALU.max))
                dve.tensor_scalar(exp_bias[:, t:t + 1], row_max[:, t:t + 1], -SCALE, None,
                                  ALU.mult).then_inc(bias_ready, 1)

            def residual(t):
                link(dve.reciprocal(inv_sum[:, t:t + 1], row_sum[:, t:t + 1]))
                link(dve.tensor_scalar(coef[:, t:t + 1], inv_sum[:, t:t + 1], gate_valid[:, t // TB:t // TB + 1], None,
                                       ALU.mult))
                dve.wait_ge(read_ready, t + 1)
                link(dve.scalar_tensor_tensor(out=x1[:, t, :], in0=bank[SCORE_BANK[t]][:, 0:D],
                                              scalar=coef[:, t:t + 1], in1=x_sb[:, t, :], op0=ALU.mult, op1=ALU.add))
                link(dve.bn_stats(stats2[:, t, :], x1[:, t, :]))
                link(dve.bn_aggr(mean_var2[:, t, :], stats2[:, t, :]))
                dve.tensor_scalar(var_eps2[:, t:t + 1], mean_var2[:, t, 1:2], EPS, None, ALU.add).then_inc(var_ready, 1)

            def normalise2(t):
                dve.wait_ge(rstd_ready, B + t + 1)
                dve.tensor_scalar(xn2[:, t, :], x1[:, t, :], mean_var2[:, t, 0:1], rstd2[:, t:t + 1],
                                  ALU.subtract, ALU.mult).then_inc(x1_ready, 1)

            maximum(0)
            maximum(1)
            maximum(2)
            low(FIRST_PT)
            maximum(3)
            low(FIRST_PT + 1)
            residual(0)
            low(FIRST_PT + 2)
            residual(1)
            normalise2(0)
            low(FIRST_PT + 3)
            normalise2(1)
            residual(2)
            residual(3)
            normalise2(2)
            normalise2(3)
            low(FIRST_F)
            low(FIRST_F + 1)

            def per_token(v):
                return v.unsqueeze(2).broadcast_to([P, NT, E])

            def per_expert(v):
                return v.unsqueeze(1).broadcast_to([P, NT, E])

            dve.wait_ge(logits_ready, 1)
            link(dve.tensor_copy(logits[:], bank[4][:, 0:NT * E].rearrange("p (t e) -> p t e", t=NT)))
            link(dve.tensor_reduce(logit_max[:], logits[:], AX.X, ALU.max))
            dve.tensor_tensor(centred[:], logits[:], per_token(logit_max[:]), ALU.subtract).then_inc(centred_ready, 1)

            def best(choice, values):
                link(dve.tensor_reduce(top[:], values, AX.X, ALU.max))
                link(dve.tensor_tensor(at_max[:], values, per_token(top[:]), ALU.is_equal))
                link(dve.tensor_tensor(at_max[:], at_max[:], per_expert(rank[:]), ALU.mult))
                link(dve.tensor_reduce(top_rank[:], at_max[:], AX.X, ALU.max))
                link(dve.tensor_tensor(choice, per_expert(rank[:]), per_token(top_rank[:]), ALU.is_equal))

            def route():
                link(dve.tensor_tensor(biased[:], logits[:], per_expert(rb_sb[:]), ALU.add))
                best(first[:], biased[:])
                link(dve.scalar_tensor_tensor(out=rest[:], in0=first[:], scalar=-1e38, in1=biased[:], op0=ALU.mult,
                                              op1=ALU.add))
                best(second[:], rest[:])
                link(dve.tensor_tensor(first[:], first[:], second[:], ALU.add))
                dve.wait_ge(expd_ready, 1)
                link(dve.tensor_reduce(total[:], expd[:], AX.X, ALU.add))
                link(dve.reciprocal(inv_total[:], total[:]))
                link(dve.tensor_tensor(expd[:], expd[:], per_token(inv_total[:]), ALU.mult))
                link(dve.tensor_tensor(expd[:], expd[:], first[:], ALU.mult))
                link(dve.tensor_reduce(total[:], expd[:], AX.X, ALU.add))
                link(dve.reciprocal(inv_total[:], total[:]))
                link(dve.tensor_tensor(comb[:, :, NS:NE], expd[:], per_token(inv_total[:]), ALU.mult))

            def gated(e, par):
                dve.wait_ge(silu_done, e + 1)
                dve.wait_ge(g_done, e + 1)
                dve.tensor_tensor(h[:, par, :], silu[:, par, :], view(G_BANK[par]), ALU.mult).then_inc(mul_done, 1)

            def h_low(e, par):
                dve.wait_ge(h_hi_done, e + 1)
                dve.tensor_tensor(h_lo[:, par, :], h[:, par, :], h_hi[:, par, :].bitcast(F32),
                                  ALU.subtract).then_inc(h_lo_done, 1)

            def accumulate(e, par):
                dve.wait_ge(y_done, e + 1)
                dve.wait_ge(acc_done, e + 1)
                for t in range(NT):
                    ins = dve.scalar_tensor_tensor(
                        out=acc[:, t, :], in0=bank[Y_BANK[par][t // 2]][:, (t % 2) * D:(t % 2) * D + D],
                        scalar=comb[:, t, bass.ds(e, 1)], in1=acc[:, t, :], op0=ALU.mult, op1=ALU.add)
                ins.then_inc(acc_done, 1)

            dve.wait_ge(consts_ready, 5)
            gated(0, 0)
            h_low(0, 0)
            route()

            def step(e, par):
                gated(e, par)
                accumulate(e - 1, 1 - par)
                h_low(e, par)

            with dve.Fori(0, (NE - 4) // 2) as i:
                step(2 * i + 1, 1)
                step(2 * i + 2, 0)
            step(NE - 3, 1)
            step(NE - 2, 0)
            step(NE - 1, 1)
            accumulate(NE - 1, 1)
            dve.wait_ge(acc_done, NE + 1)
            for t in range(NT):
                dve.scalar_tensor_tensor(out=result[:, t, :], in0=acc[:, t, :], scalar=tanh_g[:, 1:2],
                                         in1=x1[:, t, :], op0=ALU.mult, op1=ALU.add).then_inc(result_ready, 1)

        @block.tensor
        def _(pe):
            def product(dst, pairs, opened=False):
                for n, ((l_hi, l_lo), (r_hi, r_lo)) in enumerate(pairs):
                    last = n == len(pairs) - 1
                    pe.matmul(dst, l_hi, r_hi, start=(n == 0 and not opened), stop=False)
                    pe.matmul(dst, l_hi, r_lo, start=False, stop=False)
                    ins = pe.matmul(dst, l_lo, r_hi, start=False, stop=last)
                return ins

            def turn_ctx(b, k):
                for m in range(NM):
                    ins = pe.transpose(bank[2 + 2 * b + k][:, m * P:(m + 1) * P],
                                       ctx_sb[:, NM * b + m, k * P:(k + 1) * P], ident[:])
                ins.then_inc(turned, 1)

            def turn_rows(b, rows, dst):
                for k in range(NK):
                    for t in range(TB):
                        ins = pe.transpose(dst[:, k * S + t * P:k * S + (t + 1) * P],
                                           rows[:, TB * b + t, k * P:(k + 1) * P], ident[:])
                ins.then_inc(turned, 1)

            pe.wait_ge(consts_ready, 5)
            pe.wait_ge(ctx_landed[0], 16)
            turn_ctx(0, 0)
            turn_ctx(0, 1)
            pe.wait_ge(small_landed, 5 * 16)
            for k in range(NK):
                ins = pe.transpose(bank[6][:, k * E:(k + 1) * E], rw_sb[:, k * P:(k + 1) * P], ident[0:E, 0:E])
            ins.then_inc(turned, 1)
            pe.wait_ge(xn_ready, TB)
            turn_rows(0, xn, bank[0])
            pe.wait_ge(xn_ready, NT)
            turn_rows(1, xn, bank[1])
            pe.wait_ge(ctx_landed[1], 16)
            turn_ctx(1, 0)
            turn_ctx(1, 1)
            pe.wait_ge(mask_ready, 1)

            def scores(t, splits_done):
                b, c = t // TB, slice((t % TB) * P, (t % TB + 1) * P)
                pe.wait_ge(lo_ready, splits_done)
                dst = view(SCORE_BANK[t])
                pe.matmul(dst, ones_row[:], mask_bias[:, b, :], start=True, stop=False)
                product(dst, [((xT_hi[:, b, k, c], xT_lo[:, b, k, c]),
                               (ctxT_hi[:, NK * b + k, :], ctxT_lo[:, NK * b + k, :]))
                              for k in range(NK)], opened=True).then_inc(scores_ready, 1)

            def turn_probs(t):
                pe.wait_ge(probs_ready, t + 1)
                for m in range(NM):
                    ins = pe.transpose(bank[PT_BANK[t]][:, m * P:(m + 1) * P], probs[:, t, m * P:(m + 1) * P],
                                       ident[:])
                ins.then_inc(turned, 1)

            def readout(t):
                b = t // TB
                pe.wait_ge(ctx_split, b + 1)
                pe.wait_ge(lo_ready, FIRST_PT + t + 1)
                product(bank[SCORE_BANK[t]][:, 0:D],
                        [((pT_hi[:, t, m, :], pT_lo[:, t, m, :]), (ctx_hi[:, NM * b + m, :], ctx_lo[:, NM * b + m, :]))
                         for m in range(NM)]).then_inc(read_ready, 1)

            scores(0, 4)
            scores(1, 4)
            scores(2, 7)
            turn_probs(0)
            scores(3, 7)
            turn_probs(1)
            readout(0)
            turn_probs(2)
            readout(1)
            turn_probs(3)
            readout(2)
            readout(3)
            for b in range(B):
                pe.wait_ge(x1_ready, TB * (b + 1))
                turn_rows(b, xn2, bank[2 + b])
            pe.wait_ge(lo_ready, FIRST_F + B)
            for t in range(NT):
                b, c = t // TB, slice((t % TB) * P, (t % TB + 1) * P)
                ins = product(bank[4][:, t * E:(t + 1) * E],
                              [((fT_hi[:, b, k, c], fT_lo[:, b, k, c]), (rwT_hi[:, k, :], rwT_lo[:, k, :]))
                               for k in range(NK)])
            ins.then_inc(logits_ready, 1)

            def up_gate(e, par, lead=False):
                pe.wait_ge(wug_lo_done, e + 1)
                for n, (banks, freed, done) in enumerate(((U_BANK, silu_done, u_done), (G_BANK, mul_done, g_done))):
                    if not lead:
                        pe.wait_ge(freed, e - 1)
                    cols = [slice((n * NK + k) * F, (n * NK + k + 1) * F) for k in range(NK)]
                    product(view(banks[par]), [((wug_hi[:, par, cols[k]], wug_lo[:, par, cols[k]]),
                                                (fT_hi[:, :, k, :], fT_lo[:, :, k, :]))
                                               for k in range(NK)]).then_inc(done, 1)

            def down(e, par, lead=False):
                pe.wait_ge(wd_lo_done, e + 1)
                pe.wait_ge(h_lo_done, e + 1)
                if not lead:
                    pe.wait_ge(acc_done, e)
                for t in range(NT):
                    c = slice(t * P, (t + 1) * P)
                    ins = product(bank[Y_BANK[par][t // 2]][:, (t % 2) * D:(t % 2) * D + D],
                                  [((h_hi[:, par, c], h_lo[:, par, c]), (wd_hi[:, par, :], wd_lo[:, par, :]))])
                ins.then_inc(y_done, 1)

            up_gate(0, 0, lead=True)
            up_gate(1, 1, lead=True)
            down(0, 0, lead=True)
            up_gate(2, 0)
            down(1, 1, lead=True)
            with pe.Fori(0, (NE - 4) // 2) as i:
                up_gate(2 * i + 3, 1)
                down(2 * i + 2, 0)
                up_gate(2 * i + 4, 0)
                down(2 * i + 3, 1)
            up_gate(NE - 1, 1)
            down(NE - 2, 0)
            down(NE - 1, 1)


_INS = ["x", "ctx_2048", "mask_BxS2_bk0", "g_xattn", "g_ffn", "L0_ffn_router_w", "L0_ffn_router_bias", "L0_ffn_Wu",
        "L0_ffn_Wg", "L0_ffn_Wd", "L0_ffn_Su", "L0_ffn_Sg", "L0_ffn_Sd"]


def kernel(**inputs):
    import numpy as np
    import concourse.bacc as bacc
    from concourse.bass_utils import run_bass_kernel_spmd

    nc = bacc.Bacc("TRN2", target_bir_lowering=False, num_devices=1)
    arrays, args = {}, []
    for name in _INS:
        a = np.ascontiguousarray(inputs[name])
        arrays[f"in_{name}"] = a
        args.append(nc.dram_tensor(f"in_{name}", a.shape, mybir.dt.from_np(a.dtype), kind="ExternalInput").ap())
    out = nc.dram_tensor("out", arrays["in_x"].shape, F32, kind="ExternalOutput").ap()
    flamingo_block(nc, *args, out)
    r = run_bass_kernel_spmd(nc, [arrays], core_ids=[0])
    return r.results[0]["out"]
```

```python
from contextlib import ExitStack

import concourse.bass as bass
from concourse import mybir

F32 = mybir.dt.float32
F32R = mybir.dt.float32r
BF16 = mybir.dt.bfloat16
ALU = mybir.AluOpType
ACT = mybir.ActivationFunctionType
AX = mybir.AxisListType

P = 128
MASKED = -1e30
EPS = 1e-5
WARM = 32


def flamingo_block(nc, x, ctx_mem, mask, g_xattn, g_ffn, router_w, router_b, Wu, Wg, Wd, Su, Sg, Sd, out):
    B, S, D = x.shape
    M = ctx_mem.shape[1]
    E, _, F = Wu.shape
    NK = D // P
    NT = B * S // P
    TB = S // P
    NM = M // P
    NS = Su.shape[2] // F
    NE = NS + E
    WUG = 2 * NK * F
    WW = WUG + D
    assert NK == 2 and TB == 2 and F == P and NS == 2 and B == 2
    assert D & (D - 1) == 0 and D.bit_length() % 2 == 1

    x_v = x.rearrange("b (t p) d -> b p t d", p=P)
    out_v = out.rearrange("b (t p) d -> (b t) p d", p=P)
    ctx_v = ctx_mem.rearrange("b (m p) d -> b p m d", p=P)

    with ExitStack() as stack:
        def sb(name, shape, dt=F32):
            return stack.enter_context(nc.sbuf_tensor(name, shape, dt))

        def sem(name):
            return stack.enter_context(nc.semaphore(name))

        bank = [stack.enter_context(nc.psum_tensor(f"bank{i}", [P, 512], F32)) for i in range(8)]
        SCORE_BANK = [6, 7, 0, 1]
        PT_BANK = [2, 3, 4, 5]
        READ_BANK = [6, 7, 2, 3]
        F_BANK = [4, 5]
        LOGIT_BANK, TURNED_LOGIT_BANK = 4, 5
        U_BANK, G_BANK = [0, 1], [6, 7]
        Y_BANK = [[2, 3], [4, 5]]
        LAST_BANK = [4, 5, 0, 6]

        ident = sb("ident", [P, P])
        ones_row = sb("ones_row", [P, P], BF16)
        neg_half = sb("neg_half", [P, NT])
        rank = sb("rank", [P, E])
        x_sb = sb("x_sb", [P, NT, D])
        ctx_sb = sb("ctx_sb", [P, B * NM, D])
        mask_sb = sb("mask_sb", [P, B, M], mybir.dt.uint8)
        gates = sb("gates", [P, 2])
        rw_sb = sb("rw_sb", [P, D])
        rb_sb = sb("rb_sb", [P, E])
        w_raw = sb("w_raw", [P, NE, WW])
        mask_bias = sb("mask_bias", [P, B, M], BF16)
        valid = sb("valid", [P, B])
        stats = sb("stats", [P, NT, 6])
        mean_var = sb("mean_var", [P, NT, 2])
        var_eps = sb("var_eps", [P, NT])
        rstd = sb("rstd", [P, NT])
        xn = sb("xn", [P, NT, D])
        xT_hi = sb("xT_hi", [P, B, NK, S], F32R)
        xT_lo = sb("xT_lo", [P, B, NK, S], F32R)
        ctxT_hi = sb("ctxT_hi", [P, B * NK, M], F32R)
        ctxT_lo = sb("ctxT_lo", [P, B * NK, M], F32R)
        ctx_hi = sb("ctx_hi", [P, B * NM, D], F32R)
        ctx_lo = sb("ctx_lo", [P, B * NM, D], F32R)
        neg_max = sb("neg_max", [P, NT])
        probs = sb("probs", [P, NT, M])
        row_sum = sb("row_sum", [P, NT])
        inv_sum = sb("inv_sum", [P, NT])
        tanh_g = sb("tanh_g", [P, 2])
        gate_valid = sb("gate_valid", [P, B])
        coef = sb("coef", [P, NT])
        pT_hi = sb("pT_hi", [P, NT, NM, P], F32R)
        pT_lo = sb("pT_lo", [P, NT, NM, P], F32R)
        acc = sb("acc", [P, NT, D])
        stats2 = sb("stats2", [P, NT, 6])
        mean_var2 = sb("mean_var2", [P, NT, 2])
        var_eps2 = sb("var_eps2", [P, NT])
        rstd2 = sb("rstd2", [P, NT])
        xn2 = sb("xn2", [P, NT, D])
        fT_hi = sb("fT_hi", [P, B, NK, S], F32R)
        fT_lo = sb("fT_lo", [P, B, NK, S], F32R)
        rwT_hi = sb("rwT_hi", [P, NK, P], F32R)
        rwT_lo = sb("rwT_lo", [P, NK, P], F32R)
        logitsT = sb("logitsT", [E, NT * P])
        logits = sb("logits", [P, NT, E])
        biased = sb("biased", [P, NT, E])
        rest = sb("rest", [P, NT, E])
        at_max = sb("at_max", [P, NT, E])
        first = sb("first", [P, NT, E])
        second = sb("second", [P, NT, E])
        top = sb("top", [P, NT])
        top_rank = sb("top_rank", [P, NT])
        logit_max = sb("logit_max", [P, NT])
        centred = sb("centred", [P, NT, E])
        expd = sb("expd", [P, NT, E])
        total = sb("total", [P, NT])
        inv_total = sb("inv_total", [P, NT])
        comb = sb("comb", [P, NT, NE])
        wug_hi = sb("wug_hi", [P, 2, WUG], F32R)
        wug_lo = sb("wug_lo", [P, 2, WUG], F32R)
        wd_hi = sb("wd_hi", [P, 2, D], F32R)
        wd_lo = sb("wd_lo", [P, 2, D], F32R)
        silu = sb("silu", [P, 2, NT * P])
        h = sb("h", [P, 2, NT * P])
        h_hi = sb("h_hi", [P, 2, NT * P], F32R)
        h_lo = sb("h_lo", [P, 2, NT * P], F32R)

        x_landed = [sem(f"x_landed{b}") for b in range(B)]
        ctx_landed = [sem(f"ctx_landed{b}") for b in range(B)]
        mask_landed = sem("mask_landed")
        gates_landed = sem("gates_landed")
        router_landed = sem("router_landed")
        w_landed = [sem(f"w_landed{p}") for p in range(2)]
        out_stored = sem("out_stored")
        pool_step = sem("pool_step")
        ident_ready, ones_ready, rank_ready = sem("ident_ready"), sem("ones_ready"), sem("rank_ready")
        rw_cleared = sem("rw_cleared")
        mask_ready = sem("mask_ready")
        dve_step = sem("dve_step")
        var_ready = sem("var_ready")
        rstd_ready = sem("rstd_ready")
        xn_ready = sem("xn_ready")
        turned = sem("turned")
        hi_ready = sem("hi_ready")
        lo_ready = sem("lo_ready")
        ctx_split = sem("ctx_split")
        ctx_high = sem("ctx_high")
        scores_ready = sem("scores_ready")
        max_ready = sem("max_ready")
        probs_ready = sem("probs_ready")
        tanh_ready = sem("tanh_ready")
        read_ready = sem("read_ready")
        xn2_ready = sem("xn2_ready")
        logits_ready = sem("logits_ready")
        centred_ready = sem("centred_ready")
        expd_ready = sem("expd_ready")
        u_done, g_done, y_done = sem("u_done"), sem("g_done"), sem("y_done")
        silu_done, mul_done = sem("silu_done"), sem("mul_done")
        h_hi_done, h_lo_done = sem("h_hi_done"), sem("h_lo_done")
        wug_hi_done, wug_lo_done = sem("wug_hi_done"), sem("wug_lo_done")
        wd_hi_done, wd_lo_done = sem("wd_hi_done"), sem("wd_lo_done")
        acc_done = sem("acc_done")
        last_y = sem("last_y")
        last_sum = sem("last_sum")
        logits_turned = sem("logits_turned")
        logitsT_ready = sem("logitsT_ready")

        def view(i, n=512):
            return bank[i][:, 0:n]

        def flat(v):
            return v.rearrange("p a s -> p (a s)")

        splits, SPLIT = [], {}

        def split(name, src, hi, lo):
            SPLIT[name] = len(splits)
            splits.append((src, hi, lo))

        for k in range(NK):
            split(f"ctx0{k}", view(2 + k), ctxT_hi[:, k, :], ctxT_lo[:, k, :])
        split("x0", view(0), flat(xT_hi[:, 0]), flat(xT_lo[:, 0]))
        split("x1", view(1), flat(xT_hi[:, 1]), flat(xT_lo[:, 1]))
        for k in range(NK):
            split(f"ctx1{k}", view(4 + k), ctxT_hi[:, NK + k, :], ctxT_lo[:, NK + k, :])
        for name in ("p0", "p1", "p2", "f0", "p3", "router", "f1"):
            n = int(name[1]) if name != "router" else 0
            if name[0] == "p":
                split(name, view(PT_BANK[n]), flat(pT_hi[:, n]), flat(pT_lo[:, n]))
            elif name[0] == "f":
                split(name, view(F_BANK[n]), flat(fT_hi[:, n]), flat(fT_lo[:, n]))
            else:
                split(name, view(1, NK * P), flat(rwT_hi[:]), flat(rwT_lo[:]))

        block = stack.enter_context(nc.Block())

        @block.sync
        def _(sp):
            sp.dma_start(x_sb[:, 0:TB, :], x_v[0]).then_inc(x_landed[0], 16)
            sp.dma_start(x_sb[:, TB:NT, :], x_v[1]).then_inc(x_landed[1], 16)
            sp.dma_start(ctx_sb[:, 0:NM, :], ctx_v[0]).then_inc(ctx_landed[0], 16)
            sp.dma_start(ctx_sb[:, NM:2 * NM, :], ctx_v[1]).then_inc(ctx_landed[1], 16)
            for j in range(NS):
                cols = slice(j * F, (j + 1) * F)
                for n, w in enumerate((Su, Sg)):
                    sp.dma_start(w_raw[:, j, n * NK * F:(n + 1) * NK * F].rearrange("p (k f) -> p k f", k=NK),
                                 w[0, :, cols].rearrange("(k p) f -> p k f", p=P)).then_inc(w_landed[j % 2], 16)
                sp.dma_start(w_raw[:, j, WUG:WW], Sd[0, cols, :]).then_inc(w_landed[j % 2], 16)
            with sp.Fori(0, E // 2) as i:
                for par in range(2):
                    e = 2 * i + par
                    sp.wait_ge(w_landed[par], 48 * i + 48)
                    for n, w in enumerate((Wu, Wg)):
                        sp.dma_start(
                            w_raw[:, bass.ds(e + NS, 1), n * NK * F:(n + 1) * NK * F].rearrange(
                                "p o (k f) -> p (o k) f", k=NK),
                            w[bass.ds(e, 1), :, :].rearrange("o (k p) f -> p (o k) f", p=P),
                        ).then_inc(w_landed[par], 16)
                    sp.dma_start(w_raw[:, bass.ds(e + NS, 1), WUG:WW],
                                 Wd[bass.ds(e, 1), :, :].rearrange("o p d -> p o d")).then_inc(w_landed[par], 16)
            for t in range(NT):
                sp.wait_ge(last_sum, t + 1)
                sp.dma_start(out_v[t], acc[:, t, :]).then_inc(out_stored, 16)
            sp.wait_ge(out_stored, 16 * NT)

        @block.gpsimd
        def _(pool):
            pool.memset(ones_row[:], 1.0).then_inc(pool_step, 1)
            pool.wait_ge(pool_step, 1)
            pool.affine_select(out=ones_row[:], in_=ones_row[:], compare_op=ALU.is_equal, fill=0.0, base=0,
                               pattern=[[0, P]], channel_multiplier=1).then_inc(ones_ready, 1)
            pool.memset(ident[:], 1.0).then_inc(pool_step, 1)
            pool.wait_ge(pool_step, 2)
            pool.affine_select(out=ident[:], in_=ident[:], compare_op=ALU.is_equal, fill=0.0, base=0,
                               pattern=[[-1, P]], channel_multiplier=1).then_inc(ident_ready, 1)
            pool.memset(neg_half[:], -0.5).then_inc(pool_step, 1)
            pool.memset(rw_sb[:], 0.0).then_inc(rw_cleared, 1)
            pool.iota(rank[:], pattern=[[-1, E]], base=E, channel_multiplier=0,
                      allow_small_or_imprecise_dtypes=True).then_inc(rank_ready, 1)
            pool.wait_ge(pool_step, 3)
            for b in range(B):
                pool.wait_ge(var_ready, b + 1)
                pool.tensor_tensor(rstd[:, TB * b:TB * b + TB], var_eps[:, TB * b:TB * b + TB],
                                   neg_half[:, TB * b:TB * b + TB], ALU.pow).then_inc(rstd_ready, 1)
            for b in range(B):
                rows = slice(NM * b, NM * b + NM)
                pool.wait_ge(ctx_landed[b], 16)
                pool.tensor_copy(ctx_hi[:, rows, :], ctx_sb[:, rows, :]).then_inc(ctx_high, 1)
                pool.wait_ge(ctx_high, b + 1)
                pool.tensor_tensor(ctx_lo[:, rows, :], ctx_sb[:, rows, :], ctx_hi[:, rows, :].bitcast(F32),
                                   ALU.subtract).then_inc(ctx_split, 1)

            def wug_low(e, par):
                pool.wait_ge(wug_hi_done, e + 1)
                pool.tensor_tensor(wug_lo[:, par, :], w_raw[:, bass.ds(e, 1), 0:WUG],
                                   wug_hi[:, par, :].bitcast(F32), ALU.subtract).then_inc(wug_lo_done, 1)

            def wd_low(e, par):
                pool.wait_ge(wd_hi_done, e + 1)
                pool.tensor_tensor(wd_lo[:, par, :], w_raw[:, bass.ds(e, 1), WUG:WW],
                                   wd_hi[:, par, :].bitcast(F32), ALU.subtract).then_inc(wd_lo_done, 1)

            wug_low(0, 0)
            wug_low(1, 1)
            wd_low(0, 0)
            for b in range(B):
                pool.wait_ge(var_ready, B + b + 1)
                pool.tensor_tensor(rstd2[:, TB * b:TB * b + TB], var_eps2[:, TB * b:TB * b + TB],
                                   neg_half[:, TB * b:TB * b + TB], ALU.pow).then_inc(rstd_ready, 1)

            def step(e, par):
                wug_low(e + 2, par)
                wd_low(e + 1, 1 - par)

            step(0, 0)
            with pool.Fori(0, (NE - 4) // 2) as i:
                step(2 * i + 1, 1)
                step(2 * i + 2, 0)
            step(NE - 3, 1)
            wd_low(NE - 1, 1)

        @block.scalar
        def _(act):
            act.dma_start(mask_sb[:].rearrange("p b m -> p (b m)"),
                          mask.rearrange("(o b) m -> o (b m)", o=1).broadcast_to([P, B * M])).then_inc(mask_landed, 16)
            act.dma_start(gates[:, 0:1], g_xattn.rearrange("(o n) -> o n", o=1).broadcast_to([P, 1])).then_inc(gates_landed, 16)
            act.dma_start(gates[:, 1:2], g_ffn.rearrange("(o n) -> o n", o=1).broadcast_to([P, 1])).then_inc(gates_landed, 16)
            act.dma_start(rb_sb[:], router_b.rearrange("(o n) -> o n", o=1).broadcast_to([P, E])).then_inc(router_landed, 16)
            act.wait_ge(rw_cleared, 1)
            act.dma_start(rw_sb[0:E, :], router_w).then_inc(router_landed, 16)

            def high(name):
                src, hi, _ = splits[SPLIT[name]]
                act.wait_ge(turned, SPLIT[name] + 1)
                act.copy(hi, src).then_inc(hi_ready, 1)

            def exponentials(t):
                act.wait_ge(max_ready, t + 1)
                act.activation(probs[:, t, :], view(SCORE_BANK[t]), ACT.Exp, bias=neg_max[:, t:t + 1],
                               scale=1.0, accum_out=row_sum[:, t:t + 1]).then_inc(probs_ready, 1)

            def wug_high(e, par, after, count):
                act.wait_ge(w_landed[par], count)
                if after is not None:
                    act.wait_ge(g_done, after)
                act.copy(wug_hi[:, par, :], w_raw[:, bass.ds(e, 1), 0:WUG]).then_inc(wug_hi_done, 1)

            def wd_high(e, par, after):
                if after is not None:
                    act.wait_ge(y_done, after)
                act.copy(wd_hi[:, par, :], w_raw[:, bass.ds(e, 1), WUG:WW]).then_inc(wd_hi_done, 1)

            high("ctx00")
            high("ctx01")
            high("x0")
            act.wait_ge(gates_landed, 2 * 16)
            act.activation(tanh_g[:], gates[:], ACT.Tanh).then_inc(tanh_ready, 1)
            high("x1")
            high("ctx10")
            high("ctx11")
            wug_high(0, 0, None, 48)
            exponentials(0)
            wug_high(1, 1, None, 48)
            wd_high(0, 0, None)
            exponentials(1)
            high("p0")
            high("p1")
            exponentials(2)
            exponentials(3)
            high("p2")
            high("f0")
            high("p3")
            high("router")
            high("f1")
            act.wait_ge(logits_ready, 1)
            act.copy(logitsT[:], bank[LOGIT_BANK][0:E, :]).then_inc(logitsT_ready, 1)
            act.wait_ge(centred_ready, 1)
            act.activation(expd[:], centred[:], ACT.Exp).then_inc(expd_ready, 1)

            def step(e, par, landed=None, more=2, lead=False):
                act.wait_ge(u_done, e + 1)
                act.activation(silu[:, par, :], view(U_BANK[par]), ACT.Silu).then_inc(silu_done, 1)
                if more == 2:
                    wug_high(e + 2, par, e + 1, landed)
                act.wait_ge(mul_done, e + 1)
                act.copy(h_hi[:, par, :], h[:, par, :]).then_inc(h_hi_done, 1)
                if more >= 1:
                    wd_high(e + 1, 1 - par, None if lead else e)

            step(0, 0, 96, lead=True)
            with act.Fori(0, (NE - 4) // 2) as i:
                step(2 * i + 1, 1, 48 * i + 96)
                step(2 * i + 2, 0, 48 * i + 144)
            step(NE - 3, 1, 48 * (NE // 2))
            step(NE - 2, 0, more=1)
            step(NE - 1, 1, more=0)

        @block.vector
        def _(dve):
            steps = [0]

            def link(ins):
                steps[0] += 1
                ins.then_inc(dve_step, 1)
                dve.wait_ge(dve_step, steps[0])

            def low(name):
                n = SPLIT[name]
                src, hi, lo = splits[n]
                dve.wait_ge(hi_ready, n + 1)
                dve.tensor_tensor(lo, src, hi.bitcast(F32), ALU.subtract).then_inc(lo_ready, 1)

            def moments(src, b, st, mv, ve, scale):
                tiles = range(TB * b, TB * b + TB)
                for t in tiles:
                    ins = dve.bn_stats(st[:, t, :], src[:, t, :])
                link(ins)
                for t in tiles:
                    ins = dve.bn_aggr(mv[:, t, :], st[:, t, :])
                link(ins)
                both = slice(TB * b, TB * b + TB)
                dve.tensor_scalar(ve[:, both], mv[:, both, 1], EPS, scale, ALU.add, ALU.mult).then_inc(var_ready, 1)

            def normalise(src, dst, b, mv, rs, count, done):
                dve.wait_ge(rstd_ready, count)
                for t in range(TB * b, TB * b + TB):
                    dve.tensor_scalar(dst[:, t, :], src[:, t, :], mv[:, t, 0:1], rs[:, t:t + 1],
                                      ALU.subtract, ALU.mult).then_inc(done, 1)

            def maximum(t):
                dve.wait_ge(scores_ready, t + 1)
                dve.tensor_reduce(neg_max[:, t:t + 1], view(SCORE_BANK[t]), AX.X, ALU.max,
                                  negate=True).then_inc(max_ready, 1)

            def attended(t):
                dve.wait_ge(probs_ready, t + 1)
                link(dve.reciprocal(inv_sum[:, t:t + 1], row_sum[:, t:t + 1]))
                link(dve.tensor_scalar(coef[:, t:t + 1], inv_sum[:, t:t + 1], gate_valid[:, t // TB:t // TB + 1], None,
                                       ALU.mult))
                dve.wait_ge(read_ready, t + 1)
                return dve.scalar_tensor_tensor(out=acc[:, t, :], in0=bank[READ_BANK[t]][:, 0:D],
                                                scalar=coef[:, t:t + 1], in1=x_sb[:, t, :], op0=ALU.mult, op1=ALU.add)

            for b in range(B):
                dve.wait_ge(x_landed[b], 16)
                moments(x_sb, b, stats, mean_var, var_eps, float(D))
            normalise(x_sb, xn, 0, mean_var, rstd, 1, xn_ready)
            low("ctx00")
            low("ctx01")
            low("x0")
            dve.wait_ge(mask_landed, 16)
            dve.tensor_scalar(mask_bias[:], mask_sb[:], 1.0, -MASKED, ALU.subtract, ALU.mult).then_inc(mask_ready, 1)
            normalise(x_sb, xn, 1, mean_var, rstd, 2, xn_ready)
            low("x1")
            low("ctx10")
            low("ctx11")
            maximum(0)
            maximum(1)
            link(dve.tensor_reduce(valid[:], mask_sb[:], AX.X, ALU.max))
            dve.wait_ge(tanh_ready, 1)
            link(dve.tensor_scalar(gate_valid[:], valid[:], tanh_g[:, 0:1], None, ALU.mult))
            low("p0")
            low("p1")
            maximum(2)
            attended(0)
            link(attended(1))
            moments(acc, 0, stats2, mean_var2, var_eps2, 1.0)
            maximum(3)
            low("p2")
            normalise(acc, xn2, 0, mean_var2, rstd2, B + 1, xn2_ready)
            low("f0")
            low("p3")
            low("router")
            attended(2)
            link(attended(3))
            moments(acc, 1, stats2, mean_var2, var_eps2, 1.0)
            for c in range(NS):
                ins = dve.tensor_copy(comb[:, :, c], tanh_g[:, 1:2].broadcast_to([P, NT]))
            link(ins)
            normalise(acc, xn2, 1, mean_var2, rstd2, B + 2, xn2_ready)
            low("f1")

            def per_token(v):
                return v.unsqueeze(2).broadcast_to([P, NT, E])

            def per_expert(v):
                return v.unsqueeze(1).broadcast_to([P, NT, E])

            def best(choice, values):
                link(dve.tensor_reduce(top[:], values, AX.X, ALU.max))
                link(dve.tensor_tensor(at_max[:], values, per_token(top[:]), ALU.is_equal))
                link(dve.tensor_tensor(at_max[:], at_max[:], per_expert(rank[:]), ALU.mult))
                link(dve.tensor_reduce(top_rank[:], at_max[:], AX.X, ALU.max))
                link(dve.tensor_tensor(choice, per_expert(rank[:]), per_token(top_rank[:]), ALU.is_equal))

            def route():
                dve.wait_ge(rank_ready, 1)
                dve.wait_ge(router_landed, 2 * 16)
                link(dve.tensor_tensor(biased[:], logits[:], per_expert(rb_sb[:]), ALU.add))
                best(first[:], biased[:])
                link(dve.scalar_tensor_tensor(out=rest[:], in0=first[:], scalar=-1e38, in1=biased[:], op0=ALU.mult,
                                              op1=ALU.add))
                best(second[:], rest[:])
                link(dve.tensor_tensor(first[:], first[:], second[:], ALU.add))
                dve.wait_ge(expd_ready, 1)
                link(dve.tensor_reduce(total[:], expd[:], AX.X, ALU.add))
                link(dve.reciprocal(inv_total[:], total[:]))
                link(dve.tensor_tensor(expd[:], expd[:], per_token(inv_total[:]), ALU.mult))
                link(dve.tensor_tensor(expd[:], expd[:], first[:], ALU.mult))
                link(dve.tensor_reduce(total[:], expd[:], AX.X, ALU.add))
                link(dve.reciprocal(inv_total[:], total[:]))
                dve.scalar_tensor_tensor(out=comb[:, :, NS:NE], in0=expd[:], scalar=tanh_g[:, 1:2],
                                         in1=per_token(inv_total[:]), op0=ALU.mult, op1=ALU.mult).then_inc(acc_done, 1)

            def gated(e, par):
                dve.wait_ge(silu_done, e + 1)
                dve.wait_ge(g_done, e + 1)
                dve.tensor_tensor(h[:, par, :], silu[:, par, :], view(G_BANK[par]), ALU.mult).then_inc(mul_done, 1)

            def h_low(e, par):
                dve.wait_ge(h_hi_done, e + 1)
                dve.tensor_tensor(h_lo[:, par, :], h[:, par, :], h_hi[:, par, :].bitcast(F32),
                                  ALU.subtract).then_inc(h_lo_done, 1)

            def accumulate(e, par, tiles):
                dve.wait_ge(y_done, e + 1)
                dve.wait_ge(acc_done, e + 1)
                for t in tiles:
                    ins = dve.scalar_tensor_tensor(
                        out=acc[:, t, :], in0=bank[Y_BANK[par][t // 2]][:, (t % 2) * D:(t % 2) * D + D],
                        scalar=comb[:, t, bass.ds(e, 1)], in1=acc[:, t, :], op0=ALU.mult, op1=ALU.add)
                return ins

            dve.wait_ge(logits_turned, 1)
            link(dve.tensor_copy(logits[:], bank[TURNED_LOGIT_BANK][:, 0:NT * E].rearrange("p (t e) -> p t e", t=NT)))
            link(dve.tensor_reduce(logit_max[:], logits[:], AX.X, ALU.max))
            dve.tensor_tensor(centred[:], logits[:], per_token(logit_max[:]), ALU.subtract).then_inc(centred_ready, 1)
            gated(0, 0)
            h_low(0, 0)
            route()

            def step(e, par):
                gated(e, par)
                accumulate(e - 1, 1 - par, range(0, NT // 2))
                h_low(e, par)
                accumulate(e - 1, 1 - par, range(NT // 2, NT)).then_inc(acc_done, 1)

            with dve.Fori(0, (NE - 4) // 2) as i:
                step(2 * i + 1, 1)
                step(2 * i + 2, 0)
            step(NE - 3, 1)
            step(NE - 2, 0)
            step(NE - 1, 1)
            dve.wait_ge(acc_done, NE)
            for t in range(NT):
                dve.wait_ge(last_y, t + 1)
                dve.scalar_tensor_tensor(
                    out=acc[:, t, :], in0=bank[LAST_BANK[t]][:, 0:D],
                    scalar=comb[:, t, NE - 1:NE], in1=acc[:, t, :], op0=ALU.mult, op1=ALU.add).then_inc(last_sum, 1)

        @block.tensor
        def _(pe):
            def product(dst, pairs, closed=True):
                for n, ((l_hi, l_lo), (r_hi, r_lo)) in enumerate(pairs):
                    last = closed and n == len(pairs) - 1
                    pe.matmul(dst, l_hi, r_hi, start=(n == 0), stop=False)
                    pe.matmul(dst, l_hi, r_lo, start=False, stop=False)
                    ins = pe.matmul(dst, l_lo, r_hi, start=False, stop=last)
                return ins

            def turn_ctx(b, k):
                for m in range(NM):
                    ins = pe.transpose(bank[2 + 2 * b + k][:, m * P:(m + 1) * P],
                                       ctx_sb[:, NM * b + m, k * P:(k + 1) * P], ident[:])
                ins.then_inc(turned, 1)

            def turn_rows(b, rows, dst):
                for k in range(NK):
                    for t in range(TB):
                        ins = pe.transpose(dst[:, k * S + t * P:k * S + (t + 1) * P],
                                           rows[:, TB * b + t, k * P:(k + 1) * P], ident[:])
                ins.then_inc(turned, 1)

            def tokens(t):
                return t // TB, slice((t % TB) * P, (t % TB + 1) * P)

            def scores(t, last_split):
                b, c = tokens(t)
                pe.wait_ge(lo_ready, SPLIT[last_split] + 1)
                dst = view(SCORE_BANK[t])
                product(dst, [((xT_hi[:, b, k, c], xT_lo[:, b, k, c]),
                               (ctxT_hi[:, NK * b + k, :], ctxT_lo[:, NK * b + k, :]))
                              for k in range(NK)], closed=False)
                pe.wait_ge(mask_ready, 1)
                pe.matmul(dst, ones_row[:], mask_bias[:, b, :], start=False, stop=True).then_inc(scores_ready, 1)

            def turn_probs(t):
                pe.wait_ge(probs_ready, t + 1)
                for m in range(NM):
                    ins = pe.transpose(bank[PT_BANK[t]][:, m * P:(m + 1) * P], probs[:, t, m * P:(m + 1) * P],
                                       ident[:])
                ins.then_inc(turned, 1)

            def readout(t):
                b, _ = tokens(t)
                pe.wait_ge(ctx_split, b + 1)
                pe.wait_ge(lo_ready, SPLIT[f"p{t}"] + 1)
                product(bank[READ_BANK[t]][:, 0:D],
                        [((pT_hi[:, t, m, :], pT_lo[:, t, m, :]), (ctx_hi[:, NM * b + m, :], ctx_lo[:, NM * b + m, :]))
                         for m in range(NM)]).then_inc(read_ready, 1)

            pe.wait_ge(ones_ready, 1)
            for _ in range(WARM):
                pe.matmul(bank[7][:, 0:P], ones_row[:], ones_row[:], start=True, stop=True)
            pe.wait_ge(ident_ready, 1)
            pe.wait_ge(ctx_landed[0], 16)
            turn_ctx(0, 0)
            turn_ctx(0, 1)
            pe.wait_ge(xn_ready, TB)
            turn_rows(0, xn, bank[0])
            scores(0, "x0")
            pe.wait_ge(xn_ready, NT)
            turn_rows(1, xn, bank[1])
            pe.wait_ge(ctx_landed[1], 16)
            turn_ctx(1, 0)
            turn_ctx(1, 1)
            scores(1, "x0")
            turn_probs(0)
            scores(2, "ctx11")
            turn_probs(1)
            readout(0)
            scores(3, "ctx11")
            readout(1)
            turn_probs(2)
            pe.wait_ge(xn2_ready, TB)
            turn_rows(0, xn2, bank[F_BANK[0]])
            turn_probs(3)
            pe.wait_ge(router_landed, 2 * 16)
            for k in range(NK):
                ins = pe.transpose(bank[1][:, k * P:(k + 1) * P], rw_sb[:, k * P:(k + 1) * P], ident[:])
            ins.then_inc(turned, 1)
            readout(2)
            readout(3)

            def up_gate(e, par, batches=range(B), first=False):
                pe.wait_ge(wug_lo_done, e + 1)
                cut = slice(batches[0], batches[-1] + 1)
                for n, (banks, freed, done) in enumerate(((U_BANK, silu_done, u_done), (G_BANK, mul_done, g_done))):
                    if not first:
                        pe.wait_ge(freed, e - 1)
                    cols = [slice((n * NK + k) * F, (n * NK + k + 1) * F) for k in range(NK)]
                    ins = product(bank[banks[par]][:, cut.start * S:cut.stop * S],
                                  [((wug_hi[:, par, cols[k]], wug_lo[:, par, cols[k]]),
                                    (fT_hi[:, cut, k, :], fT_lo[:, cut, k, :])) for k in range(NK)])
                    if cut.stop == B:
                        ins.then_inc(done, 1)

            def down(e, par, lead=False):
                pe.wait_ge(wd_lo_done, e + 1)
                pe.wait_ge(h_lo_done, e + 1)
                if not lead:
                    pe.wait_ge(acc_done, e)
                last = isinstance(e, int) and e == NE - 1
                for t in range(NT):
                    c = slice(t * P, (t + 1) * P)
                    dst = bank[Y_BANK[par][t // 2]][:, (t % 2) * D:(t % 2) * D + D]
                    if last:
                        dst = bank[LAST_BANK[t]][:, 0:D]
                    ins = product(dst, [((h_hi[:, par, c], h_lo[:, par, c]), (wd_hi[:, par, :], wd_lo[:, par, :]))])
                    if last:
                        ins.then_inc(last_y, 1)
                if not last:
                    ins.then_inc(y_done, 1)

            pe.wait_ge(lo_ready, SPLIT["router"] + 1)
            up_gate(0, 0, batches=[0], first=True)
            up_gate(1, 1, batches=[0], first=True)
            pe.wait_ge(xn2_ready, NT)
            turn_rows(1, xn2, bank[F_BANK[1]])
            pe.wait_ge(lo_ready, SPLIT["f1"] + 1)
            up_gate(0, 0, batches=[1], first=True)
            product(view(LOGIT_BANK), [((rwT_hi[:, k, :], rwT_lo[:, k, :]), (fT_hi[:, :, k, :], fT_lo[:, :, k, :]))
                                       for k in range(NK)]).then_inc(logits_ready, 1)
            up_gate(1, 1, batches=[1], first=True)
            pe.wait_ge(logitsT_ready, 1)
            for t in range(NT):
                ins = pe.transpose(bank[TURNED_LOGIT_BANK][:, t * E:(t + 1) * E], logitsT[:, t * P:(t + 1) * P],
                                   ident[0:E, 0:E])
            ins.then_inc(logits_turned, 1)
            down(0, 0, lead=True)
            up_gate(2, 0)
            pe.wait_ge(centred_ready, 1)
            down(1, 1, lead=True)
            with pe.Fori(0, (NE - 4) // 2) as i:
                up_gate(2 * i + 3, 1)
                down(2 * i + 2, 0)
                up_gate(2 * i + 4, 0)
                down(2 * i + 3, 1)
            up_gate(NE - 1, 1)
            down(NE - 2, 0)
            down(NE - 1, 1)


_INS = ["x", "ctx_2048", "mask_BxS2_bk0", "g_xattn", "g_ffn", "L0_ffn_router_w", "L0_ffn_router_bias", "L0_ffn_Wu",
        "L0_ffn_Wg", "L0_ffn_Wd", "L0_ffn_Su", "L0_ffn_Sg", "L0_ffn_Sd"]


def kernel(**inputs):
    import numpy as np
    import concourse.bacc as bacc
    from concourse.bass_utils import run_bass_kernel_spmd

    nc = bacc.Bacc("TRN2", target_bir_lowering=False, num_devices=1)
    arrays, args = {}, []
    for name in _INS:
        a = np.ascontiguousarray(inputs[name])
        arrays[f"in_{name}"] = a
        args.append(nc.dram_tensor(f"in_{name}", a.shape, mybir.dt.from_np(a.dtype), kind="ExternalInput").ap())
    out = nc.dram_tensor("out", arrays["in_x"].shape, F32, kind="ExternalOutput").ap()
    flamingo_block(nc, *args, out)
    r = run_bass_kernel_spmd(nc, [arrays], core_ids=[0])
    return r.results[0]["out"]
```

```python
from contextlib import ExitStack

import concourse.bass as bass
from concourse import mybir

F32 = mybir.dt.float32
F32R = mybir.dt.float32r
BF16 = mybir.dt.bfloat16
ALU = mybir.AluOpType
ACT = mybir.ActivationFunctionType
AX = mybir.AxisListType

P = 128
MASKED = -2.0 ** 100
EPS = 1e-5
WARM, WARM_NORM, WARM_SPLIT = 44, 8, 20


def flamingo_block(nc, x, ctx_mem, mask, g_xattn, g_ffn, router_w, router_b, Wu, Wg, Wd, Su, Sg, Sd, out):
    B, S, D = x.shape
    M = ctx_mem.shape[1]
    E, _, F = Wu.shape
    NK = D // P
    NT = B * S // P
    TB = S // P
    NM = M // P
    NS = Su.shape[2] // F
    NE = E + NS
    WUG = 2 * NK * F
    WW = WUG + D
    LANDED = 3 * 16
    assert NK == 2 and TB == 2 and F == P and NS == 2 and B == 2
    assert D & (D - 1) == 0 and D.bit_length() % 2 == 1

    x_v = x.rearrange("b (t p) d -> b p t d", p=P)
    out_v = out.rearrange("b (t p) d -> (b t) p d", p=P)
    ctx_v = ctx_mem.rearrange("b (m p) d -> b p m d", p=P)

    with ExitStack() as stack:
        def sb(name, shape, dt=F32):
            return stack.enter_context(nc.sbuf_tensor(name, shape, dt))

        def sem(name):
            return stack.enter_context(nc.semaphore(name))

        bank = [stack.enter_context(nc.psum_tensor(f"bank{i}", [P, 512], F32)) for i in range(8)]
        SCORE_BANK = [6, 7, 0, 1]
        PT_BANK = [2, 3, 4, 5]
        READ_BANK = [6, 7, 2, 3]
        ROUTER_BANK = 2
        F_BANK = [4, 5]
        LOGIT_BANK, TURNED_LOGIT_BANK = 4, 5
        U_BANK, G_BANK = [0, 1], [6, 7]
        Y_BANK = [[2, 3], [4, 5]]
        SHARED_BANK = [0, 6, 2, 3]

        ident = sb("ident", [P, P])
        ones_row = sb("ones_row", [P, P], BF16)
        masked = sb("masked", [P, 1])
        neg_half = sb("neg_half", [P, NT])
        rank = sb("rank", [P, E])
        x_sb = sb("x_sb", [P, NT, D])
        ctx_sb = sb("ctx_sb", [P, B * NM, D])
        mask_sb = sb("mask_sb", [P, B, M], mybir.dt.uint8)
        gates = sb("gates", [P, 2])
        rw_sb = sb("rw_sb", [P, D])
        rb_sb = sb("rb_sb", [P, E])
        w_raw = sb("w_raw", [P, NE, WW])
        mask_bias = sb("mask_bias", [P, B, M], BF16)
        bias_sum = sb("bias_sum", [P, B])
        stats = sb("stats", [P, NT, 6])
        mean_var = sb("mean_var", [P, NT, 2])
        var_eps = sb("var_eps", [P, NT])
        rstd = sb("rstd", [P, NT])
        xn = sb("xn", [P, NT, D])
        xT_hi = sb("xT_hi", [P, B, NK, S], F32R)
        xT_lo = sb("xT_lo", [P, B, NK, S], F32R)
        ctxT_hi = sb("ctxT_hi", [P, B * NK, M], F32R)
        ctxT_lo = sb("ctxT_lo", [P, B * NK, M], F32R)
        ctx_hi = sb("ctx_hi", [P, B * NM, D], F32R)
        ctx_lo = sb("ctx_lo", [P, B * NM, D], F32R)
        neg_max = sb("neg_max", [P, NT])
        probs = sb("probs", [P, NT, M])
        row_sum = sb("row_sum", [P, NT])
        inv_sum = sb("inv_sum", [P, NT])
        tanh_g = sb("tanh_g", [P, 2])
        table_probe = sb("table_probe", [P, 1])
        gate_valid = sb("gate_valid", [P, B])
        coef = sb("coef", [P, NT])
        pT_hi = sb("pT_hi", [P, NT, NM, P], F32R)
        pT_lo = sb("pT_lo", [P, NT, NM, P], F32R)
        acc = sb("acc", [P, NT, D])
        stats2 = sb("stats2", [P, NT, 6])
        mean_var2 = sb("mean_var2", [P, NT, 2])
        var_eps2 = sb("var_eps2", [P, NT])
        rstd2 = sb("rstd2", [P, NT])
        fT_hi = sb("fT_hi", [P, B, NK, S], F32R)
        fT_lo = sb("fT_lo", [P, B, NK, S], F32R)
        rwT_hi = sb("rwT_hi", [P, NK, P], F32R)
        rwT_lo = sb("rwT_lo", [P, NK, P], F32R)
        logitsT = sb("logitsT", [E, NT * P])
        logits = sb("logits", [P, NT, E])
        biased = sb("biased", [P, NT, E])
        rest = sb("rest", [P, NT, E])
        at_max = sb("at_max", [P, NT, E])
        first = sb("first", [P, NT, E])
        second = sb("second", [P, NT, E])
        top = sb("top", [P, NT])
        top_rank = sb("top_rank", [P, NT])
        logit_max = sb("logit_max", [P, NT])
        centred = sb("centred", [P, NT, E])
        expd = sb("expd", [P, NT, E])
        total = sb("total", [P, NT])
        inv_total = sb("inv_total", [P, NT])
        comb = sb("comb", [P, NT, E])
        wug_hi = sb("wug_hi", [P, 4, WUG], F32R)
        wug_lo = sb("wug_lo", [P, 4, WUG], F32R)
        wd_hi = sb("wd_hi", [P, 4, D], F32R)
        wd_lo = sb("wd_lo", [P, 4, D], F32R)
        silu = sb("silu", [P, 2, NT * P])
        h = sb("h", [P, 2, NT * P])
        h_hi = sb("h_hi", [P, 4, NT * P], F32R)
        h_lo = sb("h_lo", [P, 4, NT * P], F32R)

        x_landed = [sem(f"x_landed{b}") for b in range(B)]
        ctx_landed = [sem(f"ctx_landed{b}") for b in range(B)]
        mask_landed = sem("mask_landed")
        gates_landed = sem("gates_landed")
        router_landed = sem("router_landed")
        w_landed = [sem(f"w_landed{p}") for p in range(2)]
        out_stored = sem("out_stored")
        pool_step = sem("pool_step")
        ident_ready, ones_ready, rank_ready = sem("ident_ready"), sem("ones_ready"), sem("rank_ready")
        rw_cleared = sem("rw_cleared")
        masked_ready = sem("masked_ready")
        mask_ready = sem("mask_ready")
        dve_step = sem("dve_step")
        var_ready = sem("var_ready")
        rstd_ready = sem("rstd_ready")
        xn_ready = sem("xn_ready")
        turned = sem("turned")
        hi_ready = sem("hi_ready")
        lo_ready = sem("lo_ready")
        ctx_high = sem("ctx_high")
        ctx_split = sem("ctx_split")
        scores_ready = sem("scores_ready")
        max_ready = sem("max_ready")
        probs_ready = sem("probs_ready")
        tanh_ready = sem("tanh_ready")
        read_ready = sem("read_ready")
        xn2_ready = sem("xn2_ready")
        logits_ready = sem("logits_ready")
        centred_ready = sem("centred_ready")
        expd_ready = sem("expd_ready")
        u_done, g_done, y_done = sem("u_done"), sem("g_done"), sem("y_done")
        silu_done, mul_done = sem("silu_done"), sem("mul_done")
        h_hi_done, h_lo_done = sem("h_hi_done"), sem("h_lo_done")
        wug_hi_done, wug_lo_done = sem("wug_hi_done"), sem("wug_lo_done")
        wd_hi_done, wd_lo_done = sem("wd_hi_done"), sem("wd_lo_done")
        acc_done = sem("acc_done")
        half_y = sem("half_y")
        shared_y = sem("shared_y")
        last_sum = sem("last_sum")
        logits_turned = sem("logits_turned")
        logitsT_ready = sem("logitsT_ready")

        def view(i, n=512):
            return bank[i][:, 0:n]

        def flat(v):
            return v.rearrange("p a s -> p (a s)")

        splits, SPLIT = [], {}

        def split(name, src, hi, lo):
            SPLIT[name] = len(splits)
            splits.append((src, hi, lo))

        split("ctx00", view(2), ctxT_hi[:, 0, :], ctxT_lo[:, 0, :])
        split("x0", view(0), flat(xT_hi[:, 0]), flat(xT_lo[:, 0]))
        split("ctx01", view(3), ctxT_hi[:, 1, :], ctxT_lo[:, 1, :])
        split("x1", view(1), flat(xT_hi[:, 1]), flat(xT_lo[:, 1]))
        for k in range(NK):
            split(f"ctx1{k}", view(4 + k), ctxT_hi[:, NK + k, :], ctxT_lo[:, NK + k, :])
        for name in ("p0", "p1", "p2", "p3", "f0", "router", "f1"):
            n = int(name[1]) if name != "router" else 0
            if name[0] == "p":
                split(name, view(PT_BANK[n]), flat(pT_hi[:, n]), flat(pT_lo[:, n]))
            elif name[0] == "f":
                split(name, view(F_BANK[n]), flat(fT_hi[:, n]), flat(fT_lo[:, n]))
            else:
                split(name, view(ROUTER_BANK, NK * P), flat(rwT_hi[:]), flat(rwT_lo[:]))

        block = stack.enter_context(nc.Block())

        @block.sync
        def _(sp):
            sp.dma_start(x_sb[:, 0:TB, :], x_v[0]).then_inc(x_landed[0], 16)
            sp.dma_start(x_sb[:, TB:NT, :], x_v[1]).then_inc(x_landed[1], 16)
            sp.dma_start(ctx_sb[:, 0:NM, :], ctx_v[0]).then_inc(ctx_landed[0], 16)
            sp.dma_start(ctx_sb[:, NM:2 * NM, :], ctx_v[1]).then_inc(ctx_landed[1], 16)

            def load(e, par):
                for n, w in enumerate((Wu, Wg)):
                    sp.dma_start(
                        w_raw[:, bass.ds(e, 1), n * NK * F:(n + 1) * NK * F].rearrange("p o (k f) -> p (o k) f", k=NK),
                        w[bass.ds(e, 1), :, :].rearrange("o (k p) f -> p (o k) f", p=P),
                    ).then_inc(w_landed[par], 16)
                sp.dma_start(w_raw[:, bass.ds(e, 1), WUG:WW],
                             Wd[bass.ds(e, 1), :, :].rearrange("o p d -> p o d")).then_inc(w_landed[par], 16)

            load(0, 0)
            load(1, 1)
            sp.dma_start(rb_sb[:], router_b.rearrange("(o n) -> o n", o=1).broadcast_to([P, E])).then_inc(
                router_landed, 16)
            sp.wait_ge(rw_cleared, 1)
            sp.dma_start(rw_sb[0:E, :], router_w).then_inc(router_landed, 16)
            with sp.Fori(1, E // 2) as i:
                for par in range(2):
                    sp.wait_ge(w_landed[par], LANDED * i)
                    load(2 * i + par, par)
            for j in range(NS):
                cols = slice(j * F, (j + 1) * F)
                sp.wait_ge(w_landed[j], LANDED * (E // 2))
                for n, w in enumerate((Su, Sg)):
                    sp.dma_start(w_raw[:, E + j, n * NK * F:(n + 1) * NK * F].rearrange("p (k f) -> p k f", k=NK),
                                 w[0, :, cols].rearrange("(k p) f -> p k f", p=P)).then_inc(w_landed[j], 16)
                sp.dma_start(w_raw[:, E + j, WUG:WW], Sd[0, cols, :]).then_inc(w_landed[j], 16)
            for t in range(NT):
                sp.wait_ge(last_sum, t + 1)
                sp.dma_start(out_v[t], acc[:, t, :]).then_inc(out_stored, 16)
            sp.wait_ge(out_stored, 16 * NT)

        @block.gpsimd
        def _(pool):
            pool.memset(ones_row[:], 1.0).then_inc(pool_step, 1)
            pool.wait_ge(pool_step, 1)
            pool.affine_select(out=ones_row[:], in_=ones_row[:], compare_op=ALU.is_equal, fill=0.0, base=0,
                               pattern=[[0, P]], channel_multiplier=1).then_inc(ones_ready, 1)
            pool.memset(ident[:], 1.0).then_inc(pool_step, 1)
            pool.wait_ge(pool_step, 2)
            pool.affine_select(out=ident[:], in_=ident[:], compare_op=ALU.is_equal, fill=0.0, base=0,
                               pattern=[[-1, P]], channel_multiplier=1).then_inc(ident_ready, 1)
            pool.memset(masked[:], MASKED).then_inc(masked_ready, 1)
            pool.memset(neg_half[:], -0.5).then_inc(pool_step, 1)
            pool.memset(rw_sb[:], 0.0).then_inc(rw_cleared, 1)
            pool.iota(rank[:], pattern=[[-1, E]], base=E, channel_multiplier=0,
                      allow_small_or_imprecise_dtypes=True).then_inc(rank_ready, 1)
            pool.wait_ge(pool_step, 3)
            for b in range(B):
                pool.wait_ge(var_ready, b + 1)
                pool.tensor_tensor(rstd[:, TB * b:TB * b + TB], var_eps[:, TB * b:TB * b + TB],
                                   neg_half[:, TB * b:TB * b + TB], ALU.pow).then_inc(rstd_ready, 1)
            for b in range(B):
                rows = slice(NM * b, NM * b + NM)
                pool.wait_ge(ctx_high, b + 1)
                pool.tensor_tensor(ctx_lo[:, rows, :], ctx_sb[:, rows, :], ctx_hi[:, rows, :].bitcast(F32),
                                   ALU.subtract).then_inc(ctx_split, 1)

            def wug_low(e, slot):
                pool.wait_ge(wug_hi_done, e + 1)
                pool.tensor_tensor(wug_lo[:, slot, :], w_raw[:, bass.ds(e, 1), 0:WUG],
                                   wug_hi[:, slot, :].bitcast(F32), ALU.subtract).then_inc(wug_lo_done, 1)

            def wd_low(e, slot):
                pool.wait_ge(wd_hi_done, e + 1)
                pool.tensor_tensor(wd_lo[:, slot, :], w_raw[:, bass.ds(e, 1), WUG:WW],
                                   wd_hi[:, slot, :].bitcast(F32), ALU.subtract).then_inc(wd_lo_done, 1)

            for b in range(B):
                wug_low(b, 2 + b)
                pool.wait_ge(var_ready, B + b + 1)
                pool.tensor_tensor(rstd2[:, TB * b:TB * b + TB], var_eps2[:, TB * b:TB * b + TB],
                                   neg_half[:, TB * b:TB * b + TB], ALU.pow).then_inc(rstd_ready, 1)
            wd_low(0, 2)
            wd_low(1, 3)
            wug_low(2, 0)
            wug_low(3, 1)
            wd_low(2, 0)
            wd_low(3, 1)
            wug_low(4, 0)
            wug_low(5, 1)
            with pool.Fori(2, NE // 2 - 1) as i:
                for par in range(2):
                    wug_low(2 * i + 2 + par, par)
                    wd_low(2 * i + par, par)
            wd_low(NE - 2, 2)
            wd_low(NE - 1, 3)

        @block.scalar
        def _(act):
            act.dma_start(mask_sb[:].rearrange("p b m -> p (b m)"),
                          mask.rearrange("(o b) m -> o (b m)", o=1).broadcast_to([P, B * M])).then_inc(mask_landed, 16)
            act.dma_start(gates[:, 0:1], g_xattn.rearrange("(o n) -> o n", o=1).broadcast_to([P, 1])).then_inc(
                gates_landed, 16)
            act.dma_start(gates[:, 1:2], g_ffn.rearrange("(o n) -> o n", o=1).broadcast_to([P, 1])).then_inc(
                gates_landed, 16)

            act.wait_ge(mask_landed, 16)
            act.wait_ge(masked_ready, 1)
            for b in range(B):
                act.activation(mask_bias[:, b, :], mask_sb[:, b, :], ACT.Identity, bias=masked[:], scale=-MASKED,
                               accum_out=bias_sum[:, b:b + 1]).then_inc(mask_ready, 1)

            def high(name):
                src, hi, _ = splits[SPLIT[name]]
                act.wait_ge(turned, SPLIT[name] + 1)
                act.copy(hi, src).then_inc(hi_ready, 1)

            def exponentials(t):
                act.wait_ge(max_ready, t + 1)
                act.activation(probs[:, t, :], view(SCORE_BANK[t]), ACT.Exp, bias=neg_max[:, t:t + 1],
                               scale=1.0, accum_out=row_sum[:, t:t + 1]).then_inc(probs_ready, 1)

            def wug_high(e, par, slot, after, landed):
                act.wait_ge(w_landed[par], landed)
                if after is not None:
                    act.wait_ge(g_done, after)
                act.copy(wug_hi[:, slot, :], w_raw[:, bass.ds(e, 1), 0:WUG]).then_inc(wug_hi_done, 1)

            def wd_high(e, slot, after):
                if after is not None:
                    act.wait_ge(y_done, after)
                act.copy(wd_hi[:, slot, :], w_raw[:, bass.ds(e, 1), WUG:WW]).then_inc(wd_hi_done, 1)

            def ctx_high_part(b):
                rows = slice(NM * b, NM * b + NM)
                act.wait_ge(ctx_landed[b], 16)
                act.copy(ctx_hi[:, rows, :], ctx_sb[:, rows, :]).then_inc(ctx_high, 1)

            high("ctx00")
            high("x0")
            high("ctx01")
            act.wait_ge(gates_landed, 2 * 16)
            act.activation(tanh_g[:], gates[:], ACT.Tanh).then_inc(tanh_ready, 1)
            high("x1")
            ctx_high_part(0)
            high("ctx10")
            high("ctx11")
            exponentials(0)
            ctx_high_part(1)
            high("p0")
            exponentials(1)
            high("p1")
            exponentials(2)
            wug_high(0, 0, 2, None, LANDED)
            high("p2")
            exponentials(3)
            wug_high(1, 1, 3, None, LANDED)
            high("p3")
            wd_high(0, 2, None)
            wd_high(1, 3, None)
            wug_high(2, 0, 0, None, 2 * LANDED)
            wug_high(3, 1, 1, None, 2 * LANDED)
            wd_high(2, 0, None)
            wd_high(3, 1, None)
            act.wait_ge(tanh_ready, 1)
            act.activation(table_probe[:], tanh_g[:, 0:1], ACT.Silu)
            high("f0")
            high("router")
            high("f1")

            def silu_of(e, par):
                act.wait_ge(u_done, e + 1)
                act.activation(silu[:, par, :], view(U_BANK[par]), ACT.Silu).then_inc(silu_done, 1)

            def h_high(e, par, slot, after):
                act.wait_ge(mul_done, e + 1)
                if after is not None:
                    act.wait_ge(y_done, after)
                act.copy(h_hi[:, slot, :], h[:, par, :]).then_inc(h_hi_done, 1)

            act.wait_ge(logits_ready, 1)
            act.copy(logitsT[:], bank[LOGIT_BANK][0:E, :]).then_inc(logitsT_ready, 1)
            for e in range(4):
                silu_of(e, e % 2)
                if e == 1:
                    act.wait_ge(centred_ready, 1)
                    act.activation(expd[:], centred[:], ACT.Exp).then_inc(expd_ready, 1)
                if e >= 2:
                    wug_high(e + 2, e % 2, e % 2, e + 1, 3 * LANDED)
                h_high(e, e % 2, (2, 3, 0, 1)[e], None)

            def step(e, par, landed):
                silu_of(e, par)
                wug_high(e + 2, par, par, e + 1, landed)
                h_high(e, par, par, e - 1)
                wd_high(e, par, e - 1)

            with act.Fori(2, NE // 2 - 1) as i:
                step(2 * i, 0, LANDED * i + 2 * LANDED)
                step(2 * i + 1, 1, LANDED * i + 2 * LANDED)
            for e in (NE - 2, NE - 1):
                silu_of(e, e % 2)
                wd_high(e, 2 + e % 2, None)
                h_high(e, e % 2, 2 + e % 2, None)

        @block.vector
        def _(dve):
            steps = [0]

            def link(ins):
                steps[0] += 1
                ins.then_inc(dve_step, 1)
                dve.wait_ge(dve_step, steps[0])

            def low(name):
                n = SPLIT[name]
                src, hi, lo = splits[n]
                dve.wait_ge(hi_ready, n + 1)
                dve.tensor_tensor(lo, src, hi.bitcast(F32), ALU.subtract).then_inc(lo_ready, 1)

            def moments(src, tiles, st, mv, ve, scale, meanwhile=None):
                for t in tiles:
                    ins = dve.bn_stats(st[:, t, :], src[:, t, :])
                link(ins)
                if meanwhile:
                    low(meanwhile)
                for t in tiles:
                    ins = dve.bn_aggr(mv[:, t, :], st[:, t, :])
                link(ins)
                cut = slice(tiles[0], tiles[-1] + 1)
                dve.tensor_scalar(ve[:, cut], mv[:, cut, 1], EPS, scale, ALU.add, ALU.mult).then_inc(var_ready, 1)

            def normalise(src, dst, tiles, mv, rs, count, done):
                dve.wait_ge(rstd_ready, count)
                for t in tiles:
                    dve.tensor_scalar(dst[:, t, :], src[:, t, :], mv[:, t, 0:1], rs[:, t:t + 1],
                                      ALU.subtract, ALU.mult).then_inc(done, 1)

            def maximum(t):
                dve.wait_ge(scores_ready, t + 1)
                dve.tensor_reduce(neg_max[:, t:t + 1], view(SCORE_BANK[t]), AX.X, ALU.max,
                                  negate=True).then_inc(max_ready, 1)

            def attention_weight(b):
                cut = slice(TB * b, TB * b + TB)
                dve.wait_ge(probs_ready, TB * b + TB)
                link(dve.reciprocal(inv_sum[:, cut], row_sum[:, cut]))
                link(dve.tensor_scalar(coef[:, cut], inv_sum[:, cut], gate_valid[:, b:b + 1], None, ALU.mult))

            def attended(t):
                dve.wait_ge(read_ready, t + 1)
                return dve.scalar_tensor_tensor(out=acc[:, t, :], in0=bank[READ_BANK[t]][:, 0:D],
                                                scalar=coef[:, t:t + 1], in1=x_sb[:, t, :], op0=ALU.mult, op1=ALU.add)

            FIRST, SECOND = range(TB), range(TB, NT)
            dve.wait_ge(x_landed[0], 16)
            moments(x_sb, FIRST, stats, mean_var, var_eps, float(D))
            dve.wait_ge(x_landed[1], 16)
            moments(x_sb, SECOND, stats, mean_var, var_eps, float(D))
            normalise(x_sb, xn, FIRST, mean_var, rstd, 1, xn_ready)
            normalise(x_sb, xn, SECOND, mean_var, rstd, 2, xn_ready)
            low("ctx00")
            low("x0")
            low("ctx01")
            low("x1")
            maximum(0)
            low("ctx10")
            low("ctx11")
            maximum(1)
            low("p0")
            maximum(2)
            low("p1")
            dve.wait_ge(mask_ready, B)
            dve.wait_ge(tanh_ready, 1)
            link(dve.tensor_scalar(gate_valid[:], bias_sum[:], (M - 0.5) * MASKED, tanh_g[:, 0:1], ALU.is_gt, ALU.mult))
            attention_weight(0)
            attended(0)
            maximum(3)
            low("p2")
            link(attended(1))
            moments(acc, FIRST, stats2, mean_var2, var_eps2, 1.0, meanwhile="p3")
            attention_weight(1)
            attended(2)
            normalise(acc, xn, FIRST, mean_var2, rstd2, B + 1, xn2_ready)
            link(attended(3))
            moments(acc, SECOND, stats2, mean_var2, var_eps2, 1.0)
            low("f0")
            normalise(acc, xn, SECOND, mean_var2, rstd2, B + 2, xn2_ready)
            low("router")
            low("f1")

            def per_token(v):
                return v.unsqueeze(2).broadcast_to([P, NT, E])

            def per_expert(v):
                return v.unsqueeze(1).broadcast_to([P, NT, E])

            def best(choice, values):
                link(dve.tensor_reduce(top[:], values, AX.X, ALU.max))
                link(dve.tensor_tensor(at_max[:], values, per_token(top[:]), ALU.is_equal))
                link(dve.tensor_tensor(at_max[:], at_max[:], per_expert(rank[:]), ALU.mult))
                link(dve.tensor_reduce(top_rank[:], at_max[:], AX.X, ALU.max))
                link(dve.tensor_tensor(choice, per_expert(rank[:]), per_token(top_rank[:]), ALU.is_equal))

            def route_logits():
                dve.wait_ge(logits_turned, 1)
                link(dve.tensor_copy(logits[:],
                                     bank[TURNED_LOGIT_BANK][:, 0:NT * E].rearrange("p (t e) -> p t e", t=NT)))
                link(dve.tensor_reduce(logit_max[:], logits[:], AX.X, ALU.max))
                dve.tensor_tensor(centred[:], logits[:], per_token(logit_max[:]), ALU.subtract).then_inc(
                    centred_ready, 1)

            def route_first():
                dve.wait_ge(rank_ready, 1)
                dve.wait_ge(router_landed, 2 * 16)
                link(dve.tensor_tensor(biased[:], logits[:], per_expert(rb_sb[:]), ALU.add))
                best(first[:], biased[:])

            def route_second():
                link(dve.scalar_tensor_tensor(out=rest[:], in0=first[:], scalar=-1e38, in1=biased[:], op0=ALU.mult,
                                              op1=ALU.add))
                best(second[:], rest[:])
                link(dve.tensor_tensor(first[:], first[:], second[:], ALU.add))

            def route_weights():
                dve.wait_ge(expd_ready, 1)
                link(dve.tensor_reduce(total[:], expd[:], AX.X, ALU.add))
                link(dve.reciprocal(inv_total[:], total[:]))
                link(dve.tensor_tensor(expd[:], expd[:], per_token(inv_total[:]), ALU.mult))
                link(dve.tensor_tensor(expd[:], expd[:], first[:], ALU.mult))
                link(dve.tensor_reduce(total[:], expd[:], AX.X, ALU.add))
                link(dve.reciprocal(inv_total[:], total[:]))
                link(dve.scalar_tensor_tensor(out=comb[:], in0=expd[:], scalar=tanh_g[:, 1:2],
                                              in1=per_token(inv_total[:]), op0=ALU.mult, op1=ALU.mult))

            def gated(e, par):
                dve.wait_ge(silu_done, e + 1)
                dve.wait_ge(g_done, e + 1)
                dve.tensor_tensor(h[:, par, :], silu[:, par, :], view(G_BANK[par]), ALU.mult).then_inc(mul_done, 1)

            def h_low(e, par, slot=None):
                slot = par if slot is None else slot
                dve.wait_ge(h_hi_done, e + 1)
                dve.tensor_tensor(h_lo[:, slot, :], h[:, par, :], h_hi[:, slot, :].bitcast(F32),
                                  ALU.subtract).then_inc(h_lo_done, 1)

            def accumulate(e, par, tiles, early=False):
                if early:
                    dve.wait_ge(half_y, 1)
                else:
                    dve.wait_ge(y_done, e + 1)
                if not isinstance(e, int) or e > 0:
                    dve.wait_ge(acc_done, e)
                for t in tiles:
                    ins = dve.scalar_tensor_tensor(
                        out=acc[:, t, :], in0=bank[Y_BANK[par][t // 2]][:, (t % 2) * D:(t % 2) * D + D],
                        scalar=comb[:, t, bass.ds(e, 1)], in1=acc[:, t, :], op0=ALU.mult, op1=ALU.add)
                return ins

            halves = range(0, NT // 2), range(NT // 2, NT)
            route_logits()
            gated(0, 0)
            route_first()
            h_low(0, 0, 2)
            gated(1, 1)
            route_second()
            h_low(1, 1, 3)
            gated(2, 0)
            route_weights()
            h_low(2, 0)
            accumulate(0, 0, range(NT)).then_inc(acc_done, 1)
            gated(3, 1)
            h_low(3, 1)
            accumulate(1, 1, range(NT)).then_inc(acc_done, 1)

            def step(e, par):
                gated(e, par)
                accumulate(e - 2, par, halves[0])
                h_low(e, par)
                accumulate(e - 2, par, halves[1]).then_inc(acc_done, 1)

            with dve.Fori(2, NE // 2 - 1) as i:
                step(2 * i, 0)
                step(2 * i + 1, 1)
            gated(NE - 2, 0)
            h_low(NE - 2, 0, 2)
            accumulate(NE - 4, 0, range(NT)).then_inc(acc_done, 1)
            gated(NE - 1, 1)
            accumulate(NE - 3, 1, halves[0], early=True)
            h_low(NE - 1, 1, 3)
            accumulate(NE - 3, 1, halves[1]).then_inc(acc_done, 1)
            dve.wait_ge(acc_done, E)
            for t in range(NT):
                dve.wait_ge(shared_y, t + 1)
                dve.scalar_tensor_tensor(
                    out=acc[:, t, :], in0=bank[SHARED_BANK[t]][:, 0:D],
                    scalar=tanh_g[:, 1:2], in1=acc[:, t, :], op0=ALU.mult, op1=ALU.add).then_inc(last_sum, 1)

        @block.tensor
        def _(pe):
            def product(dst, pairs, opened=True, closed=True):
                for n, ((l_hi, l_lo), (r_hi, r_lo)) in enumerate(pairs):
                    last = closed and n == len(pairs) - 1
                    pe.matmul(dst, l_hi, r_hi, start=(opened and n == 0), stop=False)
                    pe.matmul(dst, l_hi, r_lo, start=False, stop=False)
                    ins = pe.matmul(dst, l_lo, r_hi, start=False, stop=last)
                return ins

            def turn_ctx(b, k):
                for m in range(NM):
                    ins = pe.transpose(bank[2 + 2 * b + k][:, m * P:(m + 1) * P],
                                       ctx_sb[:, NM * b + m, k * P:(k + 1) * P], ident[:])
                ins.then_inc(turned, 1)

            def turn_rows(b, rows, dst):
                for k in range(NK):
                    for t in range(TB):
                        ins = pe.transpose(dst[:, k * S + t * P:k * S + (t + 1) * P],
                                           rows[:, TB * b + t, k * P:(k + 1) * P], ident[:])
                ins.then_inc(turned, 1)

            def tokens(t):
                return t // TB, slice((t % TB) * P, (t % TB + 1) * P)

            def mask_scores(t):
                b, _ = tokens(t)
                pe.wait_ge(mask_ready, b + 1)
                pe.matmul(view(SCORE_BANK[t]), ones_row[:], mask_bias[:, b, :], start=True, stop=False)

            def scores(t, needed):
                b, c = tokens(t)
                for k in range(NK):
                    if k < len(needed):
                        pe.wait_ge(lo_ready, SPLIT[needed[k]] + 1)
                    ins = product(view(SCORE_BANK[t]), [((xT_hi[:, b, k, c], xT_lo[:, b, k, c]),
                                                         (ctxT_hi[:, NK * b + k, :], ctxT_lo[:, NK * b + k, :]))],
                                  opened=False, closed=k == NK - 1)
                ins.then_inc(scores_ready, 1)

            def turn_probs(t):
                pe.wait_ge(probs_ready, t + 1)
                for m in range(NM):
                    ins = pe.transpose(bank[PT_BANK[t]][:, m * P:(m + 1) * P], probs[:, t, m * P:(m + 1) * P],
                                       ident[:])
                ins.then_inc(turned, 1)

            def readout(t):
                b, _ = tokens(t)
                pe.wait_ge(ctx_split, b + 1)
                pe.wait_ge(lo_ready, SPLIT[f"p{t}"] + 1)
                product(bank[READ_BANK[t]][:, 0:D],
                        [((pT_hi[:, t, m, :], pT_lo[:, t, m, :]), (ctx_hi[:, NM * b + m, :], ctx_lo[:, NM * b + m, :]))
                         for m in range(NM)]).then_inc(read_ready, 1)

            def keep_open(count, i):
                for _ in range(count):
                    pe.matmul(bank[i][:, 0:P], ones_row[:], ones_row[:], start=True, stop=True)

            pe.wait_ge(ones_ready, 1)
            keep_open(WARM, 7)
            pe.wait_ge(ident_ready, 1)
            pe.wait_ge(ctx_landed[0], 16)
            turn_ctx(0, 0)
            pe.wait_ge(xn_ready, TB)
            turn_rows(0, xn, bank[0])
            turn_ctx(0, 1)
            pe.wait_ge(xn_ready, NT)
            turn_rows(1, xn, bank[1])
            pe.wait_ge(ctx_landed[1], 16)
            turn_ctx(1, 0)
            turn_ctx(1, 1)
            mask_scores(0)
            mask_scores(1)
            scores(0, ("x0", "ctx01"))
            mask_scores(2)
            scores(1, ("ctx01",))
            turn_probs(0)
            scores(2, ("ctx11",))
            mask_scores(3)
            turn_probs(1)
            readout(0)
            scores(3, ("ctx11",))
            turn_probs(2)
            readout(1)
            turn_probs(3)
            readout(2)
            readout(3)
            keep_open(WARM_NORM, U_BANK[0])
            pe.wait_ge(xn2_ready, TB)
            turn_rows(0, xn, bank[F_BANK[0]])
            pe.wait_ge(router_landed, 2 * 16)
            for k in range(NK):
                ins = pe.transpose(bank[ROUTER_BANK][:, k * P:(k + 1) * P], rw_sb[:, k * P:(k + 1) * P], ident[:])
            ins.then_inc(turned, 1)
            keep_open(WARM_SPLIT, U_BANK[0])

            def up_gate(e, par, batches=range(B), first=False):
                slot = 2 + par if first else par
                pe.wait_ge(wug_lo_done, e + 1)
                cut = slice(batches[0], batches[-1] + 1)
                for n, (banks, freed, done) in enumerate(((U_BANK, silu_done, u_done), (G_BANK, mul_done, g_done))):
                    if not first:
                        pe.wait_ge(freed, e - 1)
                    cols = [slice((n * NK + k) * F, (n * NK + k + 1) * F) for k in range(NK)]
                    ins = product(bank[banks[par]][:, cut.start * S:cut.stop * S],
                                  [((wug_hi[:, slot, cols[k]], wug_lo[:, slot, cols[k]]),
                                    (fT_hi[:, cut, k, :], fT_lo[:, cut, k, :])) for k in range(NK)])
                    if cut.stop == B:
                        ins.then_inc(done, 1)

            def down(e, par, lead=False, half=False):
                slot = 2 + par if lead else par
                pe.wait_ge(wd_lo_done, e + 1)
                pe.wait_ge(h_lo_done, e + 1)
                if not lead:
                    pe.wait_ge(acc_done, e - 1)
                for t in range(NT):
                    c = slice(t * P, (t + 1) * P)
                    ins = product(bank[Y_BANK[par][t // 2]][:, (t % 2) * D:(t % 2) * D + D],
                                  [((h_hi[:, slot, c], h_lo[:, slot, c]), (wd_hi[:, slot, :], wd_lo[:, slot, :]))])
                    if half and t == NT // 2 - 1:
                        ins.then_inc(half_y, 1)
                ins.then_inc(y_done, 1)

            def down_shared(j):
                pe.wait_ge(wd_lo_done, E + j + 1)
                pe.wait_ge(h_lo_done, E + j + 1)
                for t in range(NT):
                    if j == 0 and t == 2:
                        pe.wait_ge(acc_done, E - 1)
                    c = slice(t * P, (t + 1) * P)
                    ins = product(bank[SHARED_BANK[t]][:, 0:D],
                                  [((h_hi[:, 2 + j, c], h_lo[:, 2 + j, c]), (wd_hi[:, 2 + j, :], wd_lo[:, 2 + j, :]))],
                                  opened=j == 0, closed=j == NS - 1)
                    if j == NS - 1:
                        ins.then_inc(shared_y, 1)

            pe.wait_ge(lo_ready, SPLIT["f0"] + 1)
            up_gate(0, 0, batches=[0], first=True)
            pe.wait_ge(xn2_ready, NT)
            turn_rows(1, xn, bank[F_BANK[1]])
            up_gate(1, 1, batches=[0], first=True)
            pe.wait_ge(lo_ready, SPLIT["f1"] + 1)
            product(view(LOGIT_BANK), [((rwT_hi[:, k, :], rwT_lo[:, k, :]), (fT_hi[:, :, k, :], fT_lo[:, :, k, :]))
                                       for k in range(NK)]).then_inc(logits_ready, 1)
            up_gate(0, 0, batches=[1], first=True)
            pe.wait_ge(logitsT_ready, 1)
            for t in range(NT):
                ins = pe.transpose(bank[TURNED_LOGIT_BANK][:, t * E:(t + 1) * E], logitsT[:, t * P:(t + 1) * P],
                                   ident[0:E, 0:E])
            ins.then_inc(logits_turned, 1)
            up_gate(1, 1, batches=[1], first=True)
            up_gate(2, 0)
            up_gate(3, 1)
            down(0, 0, lead=True)
            pe.wait_ge(centred_ready, 1)
            down(1, 1, lead=True)
            with pe.Fori(1, NE // 2 - 2) as i:
                up_gate(2 * i + 2, 0)
                down(2 * i, 0)
                up_gate(2 * i + 3, 1)
                down(2 * i + 1, 1)
            up_gate(NE - 2, 0)
            down(NE - 4, 0)
            up_gate(NE - 1, 1)
            down(NE - 3, 1, half=True)
            down_shared(0)
            down_shared(1)


_INS = ["x", "ctx_2048", "mask_BxS2_bk0", "g_xattn", "g_ffn", "L0_ffn_router_w", "L0_ffn_router_bias", "L0_ffn_Wu",
        "L0_ffn_Wg", "L0_ffn_Wd", "L0_ffn_Su", "L0_ffn_Sg", "L0_ffn_Sd"]


def kernel(**inputs):
    import numpy as np
    import concourse.bacc as bacc
    from concourse.bass_utils import run_bass_kernel_spmd

    nc = bacc.Bacc("TRN2", target_bir_lowering=False, num_devices=1)
    arrays, args = {}, []
    for name in _INS:
        a = np.ascontiguousarray(inputs[name])
        arrays[f"in_{name}"] = a
        args.append(nc.dram_tensor(f"in_{name}", a.shape, mybir.dt.from_np(a.dtype), kind="ExternalInput").ap())
    out = nc.dram_tensor("out", arrays["in_x"].shape, F32, kind="ExternalOutput").ap()
    flamingo_block(nc, *args, out)
    r = run_bass_kernel_spmd(nc, [arrays], core_ids=[0])
    return r.results[0]["out"]
```
